# Optimizing a Trainium2 kernel written in Bass

```python
import numpy as np
import jax
import jax.numpy as jnp

def _softmax(x, axis=-1):
    return jax.nn.softmax(x, axis=axis)

def _gelu(x):
    return jax.nn.gelu(x, approximate=True)

def _silu(x):
    return jax.nn.silu(x)

def _sigmoid(x):
    return jax.nn.sigmoid(x)

def _layernorm(x, axis=-1, eps=1e-05):
    m = jnp.mean(x, axis=axis, keepdims=True)
    v = jnp.var(x, axis=axis, keepdims=True)
    return (x - m) / jnp.sqrt(v + eps)

def _scatter_add(tgt, idx, src, axis=0):
    return tgt.at[idx].add(src)

def _segment_sum(src, seg, n):
    return jax.ops.segment_sum(src, seg, n)
kernel_name = 'mk_xattn_ffn_d2_seqx_r8_b5cb1b'

def setup_inputs(seed: int=0):
    np.random.seed(seed)
    _w = jnp.asarray

    def _rec_inputs():
        import jax
        import jax.numpy as jnp
        _rk = jax.random.key(seed)
        x = -0.0002928 + 1 * jax.random.normal(jax.random.fold_in(_rk, 1), (4, 512, 128), jnp.float32)
        _lenS = 512 - jax.random.randint(jax.random.fold_in(_rk, 7), (4,), 0, max(1, 512 // 4) + 1, jnp.int32)
        _lenS2 = 77 - jax.random.randint(jax.random.fold_in(_rk, 8), (4,), 0, max(1, 77 // 4) + 1, jnp.int32)
        _ctx_1024P = jax.random.normal(jax.random.fold_in(_rk, 11), (4, 16, 128), jnp.float32)
        _ctx_1024c = jax.random.dirichlet(jax.random.fold_in(_rk, 511), 0.3 * jnp.ones((16,), jnp.float32), (4, 77))
        _ctx_1024t = jnp.einsum('bsk,bkd->bsd', _ctx_1024c, _ctx_1024P)
        _ctx_1024t = _ctx_1024t * jax.lax.rsqrt(jnp.mean(jnp.square(_ctx_1024t)) + 1e-12) * 0.953939
        ctx_1024 = -1.39393e-06 + 0.999914 * (_ctx_1024t + 0.3 * jax.random.normal(jax.random.fold_in(_rk, 611), (4, 77, 128), jnp.float32))
        _validS = jnp.arange(512)[None, :] < _lenS[:, None]
        _validS2 = jnp.arange(77)[None, :] < _lenS2[:, None]
        _causal = jnp.tril(jnp.ones((512, 512), dtype=bool))
        mask_Bx1xSxS2_ik1 = jnp.where(jnp.broadcast_to(_validS2[:, None, None, :], (4, 1, 512, 77)), 1, 0).astype(jnp.int32)
        return (x, ctx_1024, mask_Bx1xSxS2_ik1)
    x, ctx_1024, mask_Bx1xSxS2_ik1 = _rec_inputs()

    def _L0_xattn_setup():
        import jax, jax.numpy as jnp
        import numpy as np
        D_MODEL = 128
        NUM_HEADS = 16
        D_K = D_MODEL // NUM_HEADS
        NEG_INF = -1000000000.0

        def _split_heads(x):
            B, S, _ = x.shape
            return x.reshape(B, S, NUM_HEADS, D_K).transpose(0, 2, 1, 3)
        key = jax.random.key(seed)
        ks = jax.random.split(key, 13)
        B, S = (2, 256)
        scale = 1.0 / np.sqrt(D_MODEL)
        inp = {'Query': jax.random.normal(ks[0], (B, S, D_MODEL), jnp.float32), 'Key': jax.random.normal(ks[1], (B, S, D_MODEL), jnp.float32), 'Values': jax.random.normal(ks[2], (B, S, D_MODEL), jnp.float32), 'Mask': jax.random.randint(ks[3], (B, 1, S, S), 0, 2, jnp.int32), 'W_q': jax.random.normal(ks[4], (D_MODEL, D_MODEL), jnp.float32) * scale, 'b_q': jnp.zeros((D_MODEL,), jnp.float32), 'W_k': jax.random.normal(ks[5], (D_MODEL, D_MODEL), jnp.float32) * scale, 'b_k': jnp.zeros((D_MODEL,), jnp.float32), 'W_v': jax.random.normal(ks[6], (D_MODEL, D_MODEL), jnp.float32) * scale, 'b_v': jnp.zeros((D_MODEL,), jnp.float32), 'W_o': jax.random.normal(ks[7], (D_MODEL, D_MODEL), jnp.float32) * scale, 'b_o': jnp.zeros((D_MODEL,), jnp.float32)}
        return inp
    _L0_xattn_all = _L0_xattn_setup()
    _L0_xattn_in = {k: v for k, v in _L0_xattn_all.items() if k in ('W_q', 'b_q', 'W_k', 'b_k', 'W_v', 'b_v', 'W_o', 'b_o')}
    del _L0_xattn_all

    def _L0_ffn_setup():
        import jax, jax.numpy as jnp
        import numpy as np
        B, S, H, NH, E, F = (4, 128, 128, 16, 8, 512)
        D = H // NH
        EPS = 1e-05

        def _layernorm(x, g, b):
            mu = jnp.mean(x, axis=-1, keepdims=True)
            var = jnp.var(x, axis=-1, keepdims=True)
            return (x - mu) * jax.lax.rsqrt(var + EPS) * g + b
        key = jax.random.key(seed)
        ks = jax.random.split(key, 16)
        s = 0.02
        return {'x': jax.random.normal(ks[0], (B, S, H), jnp.float32), 'ln1_g': jnp.ones((H,), jnp.float32), 'ln1_b': jnp.zeros((H,), jnp.float32), 'ln2_g': jnp.ones((H,), jnp.float32), 'ln2_b': jnp.zeros((H,), jnp.float32), 'wq': jax.random.normal(ks[1], (H, H), jnp.float32) * s, 'bq': jnp.zeros((H,), jnp.float32), 'wk': jax.random.normal(ks[2], (H, H), jnp.float32) * s, 'bk': jnp.zeros((H,), jnp.float32), 'wv': jax.random.normal(ks[3], (H, H), jnp.float32) * s, 'bv': jnp.zeros((H,), jnp.float32), 'wo': jax.random.normal(ks[4], (H, H), jnp.float32) * s, 'bo': jnp.zeros((H,), jnp.float32), 'gate_w': jax.random.normal(ks[5], (H, E), jnp.float32) * s, 'gate_b': jnp.zeros((E,), jnp.float32), 'w1': jax.random.normal(ks[6], (E, H, F), jnp.float32) * s, 'b1': jnp.zeros((E, F), jnp.float32), 'w2': jax.random.normal(ks[7], (E, F, H), jnp.float32) * s, 'b2': jnp.zeros((E, H), jnp.float32)}
    _L0_ffn_all = _L0_ffn_setup()
    _L0_ffn_in = {k: v for k, v in _L0_ffn_all.items() if k in ('ln1_g', 'ln1_b', 'ln2_g', 'ln2_b', 'wq', 'bq', 'wk', 'bk', 'wv', 'bv', 'wo', 'bo', 'gate_w', 'gate_b', 'w1', 'b1', 'w2', 'b2')}
    del _L0_ffn_all

    def _L1_xattn_setup():
        import jax, jax.numpy as jnp
        import numpy as np
        import math
        EMBED = 128
        HEADS = 16
        HEAD_DIM = EMBED // HEADS

        def alibi_slopes(heads: int) -> jnp.ndarray:
            return jnp.asarray([2.0 ** (-8.0 * (h + 1) / heads) for h in range(heads)], dtype=jnp.float32)
        key = jax.random.key(seed)
        ks = jax.random.split(key, 8)
        B, Nq, Nk = (2, 256, 256)
        s = 0.02
        return {'query': jax.random.normal(ks[0], (B, Nq, EMBED), jnp.float32), 'kv': jax.random.normal(ks[1], (B, Nk, EMBED), jnp.float32), 'Wq': jax.random.normal(ks[2], (EMBED, EMBED), jnp.float32) * s, 'bq': jnp.zeros((EMBED,), jnp.float32), 'Wkv': jax.random.normal(ks[3], (EMBED, 2 * EMBED), jnp.float32) * s, 'bkv': jnp.zeros((2 * EMBED,), jnp.float32), 'Wo': jax.random.normal(ks[4], (EMBED, EMBED), jnp.float32) * s, 'bo': jnp.zeros((EMBED,), jnp.float32)}
    _L1_xattn_all = _L1_xattn_setup()
    _L1_xattn_in = {k: v for k, v in _L1_xattn_all.items() if k in ('Wq', 'bq', 'Wkv', 'bkv', 'Wo', 'bo')}
    del _L1_xattn_all

    def _L1_ffn_setup():
        import jax, jax.numpy as jnp
        import numpy as np
        CAPACITY_FACTOR = 0.5
        key = jax.random.key(seed)
        ks = jax.random.split(key, 5)
        B, S, D, F = (4, 512, 128, 512)
        scale_in = 1.0 / np.sqrt(D)
        scale_ff = 1.0 / np.sqrt(F)
        return {'hidden_states': jax.random.normal(ks[0], (B, S, D), dtype=jnp.float32), 'w_router': jax.random.normal(ks[1], (D,), dtype=jnp.float32) * scale_in, 'W1': jax.random.normal(ks[2], (D, F), dtype=jnp.float32) * scale_in, 'b1': jnp.zeros((F,), dtype=jnp.float32), 'W2': jax.random.normal(ks[3], (F, D), dtype=jnp.float32) * scale_ff, 'b2': jnp.zeros((D,), dtype=jnp.float32)}
    _L1_ffn_all = _L1_ffn_setup()
    _L1_ffn_in = {k: v for k, v in _L1_ffn_all.items() if k in ('w_router', 'W1', 'b1', 'W2', 'b2')}
    del _L1_ffn_all
    return {'x': x, 'ctx_1024': ctx_1024, 'mask_Bx1xSxS2_ik1': mask_Bx1xSxS2_ik1, 'L0_xattn_W_q': _L0_xattn_in['W_q'], 'L0_xattn_b_q': _L0_xattn_in['b_q'], 'L0_xattn_W_k': _L0_xattn_in['W_k'], 'L0_xattn_b_k': _L0_xattn_in['b_k'], 'L0_xattn_W_v': _L0_xattn_in['W_v'], 'L0_xattn_b_v': _L0_xattn_in['b_v'], 'L0_xattn_W_o': _L0_xattn_in['W_o'], 'L0_xattn_b_o': _L0_xattn_in['b_o'], 'L0_ffn_ln1_g': _L0_ffn_in['ln1_g'], 'L0_ffn_ln1_b': _L0_ffn_in['ln1_b'], 'L0_ffn_ln2_g': _L0_ffn_in['ln2_g'], 'L0_ffn_ln2_b': _L0_ffn_in['ln2_b'], 'L0_ffn_wq': _L0_ffn_in['wq'], 'L0_ffn_bq': _L0_ffn_in['bq'], 'L0_ffn_wk': _L0_ffn_in['wk'], 'L0_ffn_bk': _L0_ffn_in['bk'], 'L0_ffn_wv': _L0_ffn_in['wv'], 'L0_ffn_bv': _L0_ffn_in['bv'], 'L0_ffn_wo': _L0_ffn_in['wo'], 'L0_ffn_bo': _L0_ffn_in['bo'], 'L0_ffn_gate_w': _L0_ffn_in['gate_w'], 'L0_ffn_gate_b': _L0_ffn_in['gate_b'], 'L0_ffn_w1': _L0_ffn_in['w1'], 'L0_ffn_b1': _L0_ffn_in['b1'], 'L0_ffn_w2': _L0_ffn_in['w2'], 'L0_ffn_b2': _L0_ffn_in['b2'], 'L1_xattn_Wq': _L1_xattn_in['Wq'], 'L1_xattn_bq': _L1_xattn_in['bq'], 'L1_xattn_Wkv': _L1_xattn_in['Wkv'], 'L1_xattn_bkv': _L1_xattn_in['bkv'], 'L1_xattn_Wo': _L1_xattn_in['Wo'], 'L1_xattn_bo': _L1_xattn_in['bo'], 'L1_ffn_w_router': _L1_ffn_in['w_router'], 'L1_ffn_W1': _L1_ffn_in['W1'], 'L1_ffn_b1': _L1_ffn_in['b1'], 'L1_ffn_W2': _L1_ffn_in['W2'], 'L1_ffn_b2': _L1_ffn_in['b2']}

def reference(x, ctx_1024, mask_Bx1xSxS2_ik1, L0_xattn_W_q, L0_xattn_b_q, L0_xattn_W_k, L0_xattn_b_k, L0_xattn_W_v, L0_xattn_b_v, L0_xattn_W_o, L0_xattn_b_o, L0_ffn_ln1_g, L0_ffn_ln1_b, L0_ffn_ln2_g, L0_ffn_ln2_b, L0_ffn_wq, L0_ffn_bq, L0_ffn_wk, L0_ffn_bk, L0_ffn_wv, L0_ffn_bv, L0_ffn_wo, L0_ffn_bo, L0_ffn_gate_w, L0_ffn_gate_b, L0_ffn_w1, L0_ffn_b1, L0_ffn_w2, L0_ffn_b2, L1_xattn_Wq, L1_xattn_bq, L1_xattn_Wkv, L1_xattn_bkv, L1_xattn_Wo, L1_xattn_bo, L1_ffn_w_router, L1_ffn_W1, L1_ffn_b1, L1_ffn_W2, L1_ffn_b2):
    import jax
    import jax.numpy as jnp

    def _L0_xattn_ref(Query, Key, Values, Mask, W_q, b_q, W_k, b_k, W_v, b_v, W_o, b_o):
        import jax, jax.numpy as jnp
        import numpy as np
        D_MODEL = 128
        NUM_HEADS = 16
        D_K = D_MODEL // NUM_HEADS
        NEG_INF = -1000000000.0

        def _split_heads(x):
            B, S, _ = x.shape
            return x.reshape(B, S, NUM_HEADS, D_K).transpose(0, 2, 1, 3)
        q = _split_heads(Query @ W_q.T + b_q)
        k = _split_heads(Key @ W_k.T + b_k)
        v = _split_heads(Values @ W_v.T + b_v)
        scores = jnp.einsum('bhqd,bhkd->bhqk', q, k) / jnp.sqrt(jnp.float32(D_K))
        scores = jnp.where(Mask == 0, jnp.float32(NEG_INF), scores)
        attn = jax.nn.softmax(scores, axis=-1)
        out = jnp.einsum('bhqk,bhkd->bhqd', attn, v)
        B, H, S, Dk = out.shape
        out = out.transpose(0, 2, 1, 3).reshape(B, S, H * Dk)
        return out @ W_o.T + b_o

    def _L0_ffn_ref(x, ln1_g, ln1_b, ln2_g, ln2_b, wq, bq, wk, bk, wv, bv, wo, bo, gate_w, gate_b, w1, b1, w2, b2):
        import jax, jax.numpy as jnp
        import numpy as np
        B, S, H, NH, E, F = (4, 128, 128, 16, 8, 512)
        D = H // NH
        EPS = 1e-05

        def _layernorm(x, g, b):
            mu = jnp.mean(x, axis=-1, keepdims=True)
            var = jnp.var(x, axis=-1, keepdims=True)
            return (x - mu) * jax.lax.rsqrt(var + EPS) * g + b
        b, s, h = x.shape
        hn = _layernorm(x, ln1_g, ln1_b)
        q = (hn @ wq + bq).reshape(b, s, NH, D).transpose(0, 2, 1, 3)
        k = (hn @ wk + bk).reshape(b, s, NH, D).transpose(0, 2, 1, 3)
        v = (hn @ wv + bv).reshape(b, s, NH, D).transpose(0, 2, 1, 3)
        scores = jnp.einsum('bhqd,bhkd->bhqk', q, k) / jnp.sqrt(jnp.float32(D))
        attn = jax.nn.softmax(scores, axis=-1)
        o = jnp.einsum('bhqk,bhkd->bhqd', attn, v)
        o = o.transpose(0, 2, 1, 3).reshape(b, s, h)
        x = x + (o @ wo + bo)
        hn2 = _layernorm(x, ln2_g, ln2_b).reshape(-1, h)
        logits = hn2 @ gate_w + gate_b
        idx = jnp.argmax(logits, axis=-1)
        mid = jax.nn.relu(jnp.einsum('th,ehf->etf', hn2, w1) + b1[:, None, :])
        y = jnp.einsum('etf,efh->eth', mid, w2) + b2[:, None, :]
        moe = y[idx, jnp.arange(hn2.shape[0])]
        return x + moe.reshape(b, s, h)

    def _L1_xattn_ref(query, kv, Wq, bq, Wkv, bkv, Wo, bo):
        import jax, jax.numpy as jnp
        import numpy as np
        import math
        EMBED = 128
        HEADS = 16
        HEAD_DIM = EMBED // HEADS

        def alibi_slopes(heads: int) -> jnp.ndarray:
            return jnp.asarray([2.0 ** (-8.0 * (h + 1) / heads) for h in range(heads)], dtype=jnp.float32)
        B, Nq, E = query.shape
        Nk = kv.shape[1]
        H, D = (HEADS, HEAD_DIM)
        q = query @ Wq + bq
        kvp = kv @ Wkv + bkv
        k, v = jnp.split(kvp, 2, axis=-1)
        q = q.reshape(B, Nq, H, D).transpose(0, 2, 1, 3)
        k = k.reshape(B, Nk, H, D).transpose(0, 2, 1, 3)
        v = v.reshape(B, Nk, H, D).transpose(0, 2, 1, 3)
        slopes = alibi_slopes(H)
        rel = jnp.abs(jnp.arange(Nk)[None, :] - jnp.arange(Nq)[:, None] - (Nk - Nq))
        bias = -slopes[:, None, None] * rel.astype(jnp.float32)
        scale = 1.0 / math.sqrt(D)
        scores = jnp.einsum('bhqd,bhkd->bhqk', q, k) * scale + bias[None]
        attn = jax.nn.softmax(scores, axis=-1)
        out = jnp.einsum('bhqk,bhkd->bhqd', attn, v)
        out = out.transpose(0, 2, 1, 3).reshape(B, Nq, E)
        return out @ Wo + bo

    def _L1_ffn_ref(hidden_states, w_router, W1, b1, W2, b2):
        import jax, jax.numpy as jnp
        import numpy as np
        CAPACITY_FACTOR = 0.5
        'Mixture-of-Depths block: route top-k tokens through an FFN inner block,\n            scatter back with sigmoid router weights; bypassed tokens pass through.'
        B, S, D = hidden_states.shape
        k = int(S * CAPACITY_FACTOR)
        scores = jnp.einsum('bsd,d->bs', hidden_states, w_router)
        top_scores, top_idx = jax.lax.top_k(scores, k)
        weights = jax.nn.sigmoid(top_scores)
        selected = jnp.take_along_axis(hidden_states, top_idx[:, :, None], axis=1)
        h = jax.nn.gelu(jnp.einsum('bkd,df->bkf', selected, W1) + b1)
        processed = jnp.einsum('bkf,fd->bkd', h, W2) + b2
        update = weights[:, :, None] * processed

        def scatter_one(xb, ib, ub):
            return xb.at[ib].add(ub)
        output = jax.vmap(scatter_one)(hidden_states, top_idx, update)
        return output
    x = x + _L0_xattn_ref(_layernorm(x, axis=-1), ctx_1024, ctx_1024, mask_Bx1xSxS2_ik1, L0_xattn_W_q, L0_xattn_b_q, L0_xattn_W_k, L0_xattn_b_k, L0_xattn_W_v, L0_xattn_b_v, L0_xattn_W_o, L0_xattn_b_o)
    x = x + _L0_ffn_ref(_layernorm(x, axis=-1), L0_ffn_ln1_g, L0_ffn_ln1_b, L0_ffn_ln2_g, L0_ffn_ln2_b, L0_ffn_wq, L0_ffn_bq, L0_ffn_wk, L0_ffn_bk, L0_ffn_wv, L0_ffn_bv, L0_ffn_wo, L0_ffn_bo, L0_ffn_gate_w, L0_ffn_gate_b, L0_ffn_w1, L0_ffn_b1, L0_ffn_w2, L0_ffn_b2)
    x = x + _L1_xattn_ref(_layernorm(x, axis=-1), ctx_1024, L1_xattn_Wq, L1_xattn_bq, L1_xattn_Wkv, L1_xattn_bkv, L1_xattn_Wo, L1_xattn_bo)
    x = x + _L1_ffn_ref(_layernorm(x, axis=-1), L1_ffn_w_router, L1_ffn_W1, L1_ffn_b1, L1_ffn_W2, L1_ffn_b2)
    return x

_drawn_inputs = setup_inputs


def setup_inputs(seed=0):
    import zlib

    import numpy as np

    out = dict(_drawn_inputs(seed))
    spreads = {'L0_xattn_b_q': (0.0, 0.341),
     'L0_xattn_b_k': (0.0, 0.8),
     'L0_xattn_b_v': (0.0, 0.1),
     'L0_xattn_b_o': (0.0, 0.1),
     'L0_ffn_ln1_g': (1.0, 0.6),
     'L0_ffn_ln1_b': (0.0, 0.8),
     'L0_ffn_ln2_g': (1.0, 0.2),
     'L0_ffn_ln2_b': (0.0, 0.411),
     'L0_ffn_bq': (0.0, 0.8),
     'L0_ffn_bk': (0.0, 0.8),
     'L0_ffn_bv': (0.0, 0.55),
     'L0_ffn_bo': (0.0, 0.1),
     'L0_ffn_gate_b': (0.0, 0.1),
     'L0_ffn_b1': (0.0, 0.514),
     'L0_ffn_b2': (0.0, 0.1),
     'L1_xattn_bq': (0.0, 0.8),
     'L1_xattn_bkv': (0.0, 0.695),
     'L1_xattn_bo': (0.0, 0.1),
     'L1_ffn_b1': (0.0, 0.8),
     'L1_ffn_b2': (0.0, 0.584)}
    factors = {'L0_ffn_wq': 8.0,
     'L0_ffn_wk': 8.0,
     'L0_ffn_wv': 3.373,
     'L0_ffn_wo': 2.786,
     'L1_xattn_Wq': 8.0,
     'L1_xattn_Wkv': 4.504,
     'L1_xattn_Wo': 3.19}
    for name, (base, spread) in spreads.items():
        noise = np.random.default_rng([zlib.crc32(name.encode()), seed]).standard_normal(out[name].shape)
        drawn = base * np.exp(spread * noise) if base else spread * noise
        out[name] = jnp.asarray(drawn.astype(out[name].dtype))
    for name, factor in factors.items():
        out[name] = (out[name] * factor).astype(out[name].dtype)
    return out
```

```python
from contextlib import ExitStack

import concourse.bass as bass
from concourse import mybir

F32 = mybir.dt.float32
BF16 = mybir.dt.bfloat16
I32 = mybir.dt.int32
ALU = mybir.AluOpType
ACT = mybir.ActivationFunctionType
AX = mybir.AxisListType

B, S, D, SC = 4, 512, 128, 77
H = 16
DK = D // H
P = 128
NT = S // P
G, HG = 4, 4
NE, F = 8, 512
NF = F // P
TOPK = S // 2
EPS = 1e-5
PROD = 9 * DK
ALIBI = 6
CORNER = S - (S - SC) - 1
BIG = 2.0 ** 60
QSCALE = DK ** -0.5

W_NAMES = ["q0", "k0", "v0", "o0", "q1", "k1", "v1", "o1", "q2", "k2", "v2", "o2"]
C_NAMES = ["bq0", "bk0", "bq1", "bk1", "bq2", "bk2", "g1", "c1", "g2", "c2"]
R_NAMES = ["bv0", "bo0", "bv1", "bo1", "bv2", "bo2", "fb2", "router"]

MAXES = [G * NT, H * NT, G * NT]
MAX0 = [0, MAXES[0], MAXES[0] + MAXES[1]]
N_MAX = sum(MAXES)
EXPS = [2 * G, 2 * G * NT, 2 * G]
EXP0 = [0, EXPS[0], EXPS[0] + EXPS[1]]
N_EXP = sum(EXPS)
PV0 = [e // 2 for e in EXP0]
N_PV = N_EXP // 2
ROWS0 = [0, 1, 1 + G]
N_ROWS = 2 + G
MAXROW = [PROD + ALIBI, PROD, PROD + ALIBI]
LEAD = 8


def self_plan():
    plan, taken = [], 0

    def take(n):
        nonlocal taken
        for _ in range(n):
            if taken < MAXES[1]:
                plan.append(("max", taken))
                taken += 1
                if taken % (HG * NT) == 0:
                    plan.append(("parts", taken // (HG * NT) - 1))
            elif taken < MAXES[1] + LEAD:
                taken += 1
            if taken >= HG * NT and taken % (HG * NT) == 3:
                plan.append(("rows", taken // (HG * NT) - 1))

    take(HG * NT + LEAD)
    steps = EXPS[1]
    for s in range(steps + 5):
        if s < steps:
            plan.append(("exp", s))
            take(2)
        if s >= 3 and s % 2 == 1 and (s - 3) // 2 < steps // 2:
            plan.append(("pv", (s - 3) // 2))
        if s >= 5 and (s - 4) % (2 * NT) == 2 * NT - 1 + 0 and (s - 4) // (2 * NT) < G:
            plan.append(("heads", (s - 4) // (2 * NT)))
    done = [n for k, n in plan if k == "heads"]
    for g in range(G):
        if g not in done:
            plan.append(("heads", g))
    return plan


def cross_plan():
    plan = [("max", u) for u in range(G * NT)] + [("parts", 0), ("rows", 0)]
    for s in range(2 * G):
        plan.append(("exp", s))
        if s >= 3 and s % 2 == 1:
            plan.append(("pv", (s - 3) // 2))
        if s >= 4 and s % 2 == 0:
            plan.append(("heads", (s - 4) // 2))
    plan += [("pv", G - 1), ("heads", G - 2), ("heads", G - 1)]
    return plan


PLANS = [cross_plan(), self_plan(), cross_plan()]


def build(nc, t):
    ctx = ExitStack()

    def sb(name, shape, dt=F32):
        return ctx.enter_context(nc.sbuf_tensor(name, shape, dt))

    def bank(name, n=1):
        return ctx.enter_context(nc.psum_tensor(name, [P, n, 512], F32))

    def sem(name):
        return ctx.enter_context(nc.semaphore(name))

    with ctx:
        w_sb = sb("w_sb", [P, len(W_NAMES), D])
        W = {n: w_sb[:, k, :] for k, n in enumerate(W_NAMES)}
        c_sb = sb("c_sb", [P, len(C_NAMES)])
        C = {n: c_sb[:, k:k + 1] for k, n in enumerate(C_NAMES)}
        r_sb = sb("r_sb", [P, len(R_NAMES), D])
        R = {n: r_sb[:, k, :] for k, n in enumerate(R_NAMES)}
        gate_w = sb("gate_w", [P, NE])
        gate_b = sb("gate_b", [P, NE])
        w1 = sb("w1", [P, NE, F])
        b1 = sb("b1", [P, NE, NF])
        w2 = sb("w2", [P, NE, NF, D])
        b2 = sb("b2", [NE, D])
        fw1 = sb("fw1", [P, F])
        fb1 = sb("fb1", [P, NF])
        fw2 = sb("fw2", [P, NF, D])
        ident = sb("ident", [P, P])
        identb = sb("identb", [P, P], BF16)
        eye4 = sb("eye4", [SC, HG, SC], BF16)
        lower = sb("lower", [P, P])
        falling = sb("falling", [P, NE])
        halfneg = sb("halfneg", [P, NT])
        slopes = sb("slopes", [SC, 3, H, SC], BF16)
        corner = sb("corner", [SC, P], BF16)

        x0 = sb("x0", [P, NT, D])
        x1 = sb("x1", [P, NT, D])
        x2 = sb("x2", [P, NT, D])
        x3 = sb("x3", [P, NT, D])
        y = sb("y", [P, NT, D])
        res = sb("res", [P, NT, D])
        out_sb = sb("out_sb", [P, NT, D])
        z = sb("z", [P, 2, NT, D])
        zT = sb("zT", [P, S])
        stats = sb("stats", [P, NT, 6])
        meanvar = sb("meanvar", [P, NT, 2])
        vareps = sb("vareps", [P, NT])
        rstd = sb("rstd", [P, NT])
        qf = sb("qf", [P, S])
        qr = sb("qr", [P, S])
        qp = sb("qp", [P, 3, S], BF16)
        kf = sb("kf", [P, S])
        kr = sb("kr", [P, S])
        kp = sb("kp", [P, 3, S], BF16)
        qst_cross = sb("qst_cross", [MAXROW[2] + 3, H, S], BF16)
        qst = [qst_cross, sb("qst_self", [MAXROW[1] + 3, H, S], BF16), qst_cross]
        nk = [SC, S, SC]
        kst = [sb(f"kst{a}", [MAXROW[a] + 3, H, nk[a]], BF16) for a in range(3)]
        vx = [sb("vx0", [SC, 1, H, 32]), sb("vx1", [P, NT, H, 32]), sb("vx2", [SC, 1, H, 32])]
        ctx_in = sb("ctx_in", [SC, D])
        ctxT = sb("ctxT", [P, SC])
        kc = sb("kc", [P, 2, SC])
        kcr = sb("kcr", [P, 2, SC])
        kcp = sb("kcp", [P, 3, 2, SC], BF16)
        mask_in = sb("mask_in", [P, NT, SC], I32)
        mask_neg = sb("mask_neg", [P, NT, SC], BF16)
        maskT = sb("maskT", [SC, S], BF16)
        negmax = sb("negmax", [P, NT, H])
        negrest = sb("negrest", [P, NT, H])
        negp = sb("negp", [P, NT, 3, H], BF16)
        mT = sb("mT", [3 * H, S], BF16)
        probs = sb("probs", [P, 4, 2, S])
        strips = sb("strips", [P, S])
        rden = sb("rden", [P, NT, HG])
        o = sb("o", [P, NT, D])
        oT = sb("oT", [P, S])
        mid = sb("mid", [P, 2, NF, S])
        logit = sb("logit", [P, NT, NE])
        top = sb("top", [P, NT])
        hot = sb("hot", [P, NT, NE])
        pick = sb("pick", [P, NT, NE])
        hotT = sb("hotT", [NE, S])
        score = sb("score", [P, NT])
        junk = sb("junk", [P, S])
        counts = sb("counts", [P, NT, 3])
        rank = sb("rank", [P, NT])
        esig = sb("esig", [P, NT])
        weight = sb("weight", [P, NT])

        ex = [bank("ex0", 2), bank("ex1", 2)]
        mx = [bank("mx0"), bank("mx1")]
        pv = bank("pv")
        misc = bank("misc")
        misc_b = misc[:, 0, 0:256].bitcast(BF16)

        counted = {
            "sync": """x_loaded ctx_loaded mask_loaded kctx_filled q_filled k_filled rows_filled stored""",
            "tensor": """ctxT_psum kvctx_psum maskT_psum zT_psum q_psum k_psum v_psum max_scores rows_psum scores
                pv_done heads_psum oT_psum attn_psum logit_psum hotT_psum b2_psum up down rowscore_psum fup fdown""",
            "scalar": """ctxT_ready maskT_ready zT_ready rows_ready probs_ready strips_ready oT_ready hotT_ready
                mid_act sig_ready fmid""",
            "vector": """kctx_parts vctx_ready mask_num var_ready z_ready q_parts k_parts v_ready max_taken max_parts
                heads_ready attn_ready hot_ready acc_ready mid_dve down_used score_ready out_ready dve_chain""",
            "gpsimd": """rstd_ready res_ready""",
        }
        s = {n: sem(n) for names in counted.values() for n in names.split()}
        s.update({n: sem(n) for n in ("consts", "padded", "pool_chain")})

        def start_at_one(eng, name):
            for n in counted[name].split():
                eng.sem_inc(s[n], 1)

        block = ctx.enter_context(nc.Block())

        N_CONST = 27
        LN = 6

        @block.sync
        def _(sp):
            for dst, name in [(w_sb, "w"), (c_sb, "c"), (gate_w, "gate_w"), (ident, "ident"), (identb, "identb"),
                              (eye4, "eye4"), (slopes, "slopes"), (corner, "corner"), (lower, "lower"),
                              (falling, "falling"), (halfneg, "halfneg"), (fb1, "fb1"), (b1, "b1"), (b2, "b2")]:
                sp.dma_start(dst[:], t[name]).then_inc(s["consts"], 16)
            sp.dma_start(r_sb[:], t["r"].partition_broadcast(P)).then_inc(s["consts"], 16)
            sp.dma_start(gate_b[:], t["gate_b"].partition_broadcast(P)).then_inc(s["consts"], 16)
            sp.dma_start(kst[0][PROD:PROD + ALIBI], t["kzeros"]).then_inc(s["consts"], 16)
            sp.dma_start(kst[0][MAXROW[0]:MAXROW[0] + 3], t["kones"][:, :, 0:SC]).then_inc(s["consts"], 16)
            sp.dma_start(kst[1][PROD:PROD + 3], t["kones"]).then_inc(s["consts"], 16)
            sp.dma_start(kst[2][PROD:PROD + ALIBI], t["kalibi"]).then_inc(s["consts"], 16)
            sp.dma_start(kst[2][MAXROW[2]:MAXROW[2] + 3], t["kones"][:, :, 0:SC]).then_inc(s["consts"], 16)
            sp.dma_start(qst[2][PROD:PROD + ALIBI], t["qalibi"]).then_inc(s["consts"], 16)
            sp.dma_start(fw1[:], t["fw1"]).then_inc(s["consts"], 16)
            sp.dma_start(fw2[:], t["fw2"]).then_inc(s["consts"], 16)
            sp.dma_start(w1[:], t["w1"]).then_inc(s["consts"], 16)
            sp.dma_start(w2[:, 0:4], t["w2"][:, 0:4]).then_inc(s["consts"], 16)
            sp.dma_start(w2[:, 4:8], t["w2"][:, 4:8]).then_inc(s["consts"], 16)

            start_at_one(sp, "sync")

            def spread(dst, parts, filled, part_is_query):
                for i3 in range(3):
                    for j3 in range(3):
                        row = (i3 * 3 + j3) * DK
                        p3 = i3 if part_is_query else j3
                        sp.dma_start(dst[row:row + DK].rearrange("d h t -> d (h t)"), parts(p3))\
                          .then_inc(s[filled], 16)

            with sp.Fori(0, B) as i:
                sp.wait_ge(s["ctxT_psum"], 1 + i)
                sp.wait_ge(s["mask_num"], 1 + i)
                sp.wait_ge(s["res_ready"], 1 + i * 3)
                sp.dma_start(x0[:], t["x"][bass.ds(i, 1)].rearrange("o (t p) d -> p (o t) d", p=P))\
                  .then_inc(s["x_loaded"], 16)
                sp.dma_start(ctx_in[:], t["ctx"][bass.ds(i, 1)].rearrange("o k d -> (o k) d")).then_inc(s["ctx_loaded"], 16)
                sp.dma_start(mask_in[:], t["mask"][bass.ds(i, 1)].rearrange("o e (t p) k -> p (o e t) k", p=P))\
                  .then_inc(s["mask_loaded"], 16)
                sp.wait_ge(s["kctx_parts"], 1 + i + 1)
                for layer in range(2):
                    spread(kst[2 * layer], lambda p3: kcp[:, p3, layer, :], "kctx_filled", False)
                for a in range(3):
                    sp.wait_ge(s["q_parts"], 1 + 3 * i + a + 1)
                    spread(qst[a], lambda p3: qp[:, p3, :], "q_filled", True)
                    if a == 1:
                        sp.wait_ge(s["k_parts"], 1 + i + 1)
                        spread(kst[1], lambda p3: kp[:, p3, :], "k_filled", False)
                    for kind, n in PLANS[a]:
                        if kind == "rows":
                            nh, h0 = (HG, n * HG) if a == 1 else (H, 0)
                            sp.wait_ge(s["rows_ready"], 1 + N_ROWS * i + ROWS0[a] + n + 1)
                            sp.dma_start(qst[a][MAXROW[a]:MAXROW[a] + 3, h0:h0 + nh].rearrange("p h t -> p (h t)"),
                                         mT[0:3 * nh, :]).then_inc(s["rows_filled"], 16)
                sp.wait_ge(s["out_ready"], 1 + NT * i + NT)
                sp.dma_start(t["out"][bass.ds(i, 1)].rearrange("o (t p) d -> p (o t) d", p=P), out_sb[:])\
                  .then_inc(s["stored"], 16)
            sp.wait_ge(s["stored"], 1 + 16 * B)

        @block.gpsimd
        def _(pool):
            start_at_one(pool, "gpsimd")
            for a in range(3):
                nc.gpsimd.memset(vx[a][:], 0.0).then_inc(s["pool_chain"], 1)
            pool.wait_ge(s["pool_chain"], 3)
            for a in range(3):
                nc.gpsimd.memset(vx[a][:, :, :, DK:DK + 1], 1.0).then_inc(s["padded"], 1)
            pool.wait_ge(s["consts"], 16 * N_CONST)

            def rstd_of(i, n):
                pool.wait_ge(s["var_ready"], 1 + LN * i + n + 1)
                nc.gpsimd.tensor_tensor(rstd[:], vareps[:], halfneg[:], ALU.pow).then_inc(s["rstd_ready"], 1)

            def residual(i, n, x, bias):
                pool.wait_ge(s["attn_ready"], 1 + 3 * i + n)
                nc.gpsimd.tensor_tensor(res[:], x, R[bias].unsqueeze(1).to_broadcast([P, NT, D]), ALU.add)\
                    .then_inc(s["res_ready"], 1)

            with pool.Fori(0, B) as i:
                pool.wait_ge(s["x_loaded"], 1 + 16 * i + 16)
                rstd_of(i, 0)
                residual(i, 0, x0[:], "bo0")
                rstd_of(i, 1)
                pool.wait_ge(s["z_ready"], 1 + LN * i + 2)
                residual(i, 1, z[:, 1], "bo1")
                rstd_of(i, 2)
                rstd_of(i, 3)
                rstd_of(i, 4)
                residual(i, 2, x2[:], "bo2")
                rstd_of(i, 5)

        @block.scalar
        def _(act):
            start_at_one(act, "scalar")
            act.wait_ge(s["consts"], 16 * N_CONST)

            def zT_copy(i, n, g=None, c=None):
                act.wait_ge(s["zT_psum"], 1 + 5 * i + n + 1)
                if g:
                    nc.scalar.activation(zT[:], misc[:, 0, :], ACT.Identity, bias=C[c], scale=C[g])\
                        .then_inc(s["zT_ready"], 1)
                else:
                    nc.scalar.activation(zT[:], misc[:, 0, :], ACT.Copy).then_inc(s["zT_ready"], 1)

            def attention(i, a):
                for kind, n in PLANS[a]:
                    if kind == "rows":
                        nh = HG if a == 1 else H
                        e = N_ROWS * i + ROWS0[a] + n
                        act.wait_ge(s["rows_psum"], 1 + e + 1)
                        act.wait_ge(s["rows_filled"], 1 + 16 * e)
                        nc.scalar.activation(mT[0:3 * nh, :], misc_b[0:3 * nh, :], ACT.Copy)\
                            .then_inc(s["rows_ready"], 1)
                    elif kind == "exp":
                        e = EXP0[a] + n
                        act.wait_ge(s["scores"], 1 + N_EXP * i + e + 1)
                        act.wait_ge(s["pv_done"], 1 + N_PV * i + max((e - 4) // 2 + 1, 0))
                        act_rows = SC if a != 1 else P
                        nc.scalar.activation(probs[0:act_rows, e % 4], ex[e % 2][0:act_rows], ACT.Exp)\
                            .then_inc(s["probs_ready"], 1)
                    elif kind == "heads":
                        last = N_PV * i + PV0[a] + (n + 1) * (NT if a == 1 else 1)
                        act.wait_ge(s["pv_done"], 1 + last)
                        act.wait_ge(s["heads_psum"], 1 + 3 * G * i + G * a + n)
                        nc.scalar.activation(strips[:], pv[:, 0, :], ACT.Copy).then_inc(s["strips_ready"], 1)
                act.wait_ge(s["oT_psum"], 1 + 3 * i + a + 1)
                nc.scalar.activation(oT[:], misc[:, 0, :], ACT.Copy).then_inc(s["oT_ready"], 1)

            with act.Fori(0, B) as i:
                act.wait_ge(s["ctxT_psum"], 1 + i + 1)
                nc.scalar.activation(ctxT[:], misc[:, 0, 0:SC], ACT.Copy).then_inc(s["ctxT_ready"], 1)
                act.wait_ge(s["maskT_psum"], 1 + i + 1)
                nc.scalar.activation(maskT[:], misc_b[0:SC, :], ACT.Copy).then_inc(s["maskT_ready"], 1)
                zT_copy(i, 0)
                attention(i, 0)
                zT_copy(i, 1, "g1", "c1")
                attention(i, 1)
                zT_copy(i, 2, "g2", "c2")
                act.wait_ge(s["hotT_psum"], 1 + i + 1)
                nc.scalar.activation(hotT[:], pv[0:NE, 0, :], ACT.Copy).then_inc(s["hotT_ready"], 1)
                for e in range(NE):
                    act.wait_ge(s["up"], 1 + 2 * NE * i + 2 * e + 1)
                    act.wait_ge(s["down"], 1 + NE * i + max(e - 1, 0))
                    for f in range(2):
                        ins = nc.scalar.activation(mid[:, e % 2, f], ex[0][:, f], ACT.Relu, bias=b1[:, e, f:f + 1])
                    ins.then_inc(s["mid_act"], 1)
                zT_copy(i, 3)
                attention(i, 2)
                zT_copy(i, 4)
                act.wait_ge(s["score_ready"], 1 + i + 1)
                nc.scalar.activation(esig[:], score[:], ACT.Exp, scale=-1.0).then_inc(s["sig_ready"], 1)
                for f in range(NF):
                    act.wait_ge(s["fup"], 1 + NF * i + f + 1)
                    nc.scalar.activation(mid[:, 0, f], ex[f // 2][:, f % 2], ACT.Gelu_apprx_tanh,
                                         bias=fb1[:, f:f + 1]).then_inc(s["fmid"], 1)

        @block.tensor
        def _(pe):
            start_at_one(pe, "tensor")
            pe.wait_ge(s["consts"], 16 * N_CONST)
            pe.wait_ge(s["padded"], 3)

            def transposes(i, n, slot):
                pe.wait_ge(s["z_ready"], 1 + LN * i + [0, 2, 3, 4, 5][n] + 1)
                for k in range(NT):
                    ins = nc.tensor.transpose(misc[:, 0, k * P:(k + 1) * P], z[:, slot, k, :], ident[:])
                ins.then_inc(s["zT_psum"], 1)

            def project(i, a):
                pe.wait_ge(s["zT_ready"], 1 + 5 * i + [0, 1, 3][a] + 1)
                nc.tensor.matmul(mx[0][:, 0, :], W[f"q{a}"], zT[:], start=True, stop=True).then_inc(s["q_psum"], 1)
                if a == 1:
                    nc.tensor.matmul(mx[1][:, 0, :], W["k1"], zT[:], start=True, stop=True).then_inc(s["k_psum"], 1)
                    for k in range(NT):
                        ins = nc.tensor.matmul(pv[:, 0, k * P:(k + 1) * P], zT[:, k * P:(k + 1) * P], W["v1"],
                                               start=True, stop=True, skip_group_check=True)
                    ins.then_inc(s["v_psum"], 1)

            def max_tile(i, a, u):
                e = MAX0[a] + u
                pe.wait_ge(s["max_taken"], 1 + N_MAX * i + max(e - 1, 0))
                dst = mx[e % 2][:, 0, :]
                if a == 1:
                    h, k = divmod(u, NT)
                    ins = nc.tensor.matmul(dst, qst[1][0:PROD, h, k * P:(k + 1) * P], kst[1][0:PROD, h, :],
                                           start=True, stop=True)
                else:
                    g, k = divmod(u, NT)
                    rows = PROD + (ALIBI if a == 2 else 0)
                    first = True
                    if a == 0:
                        nc.tensor.matmul(dst[:, 0:HG * SC], maskT[:, k * P:(k + 1) * P], eye4[:],
                                         start=True, stop=False, skip_group_check=True)
                        first = False
                    elif k == NT - 1:
                        for part in range(3):
                            nc.tensor.matmul(dst[:, 0:HG * SC], corner[:], slopes[:, part, g * HG:(g + 1) * HG, :],
                                             start=(part == 0), stop=False, skip_group_check=True)
                        first = False
                    for c in range(HG):
                        h = g * HG + c
                        ins = nc.tensor.matmul(dst[:, c * SC:(c + 1) * SC], qst[a][0:rows, h, k * P:(k + 1) * P],
                                               kst[a][0:rows, h, :], start=first and c == 0, stop=True,
                                               skip_group_check=True)
                ins.then_inc(s["max_scores"], 1)

            def exp_tile(i, a, n):
                e = EXP0[a] + n
                pe.wait_ge(s["probs_ready"], 1 + N_EXP * i + max(e - 1, 0))
                rows = MAXROW[a] + 3
                if a == 1:
                    g, k, pair = n // (2 * NT), n % (2 * NT) // 2, n % 2
                    if n % (2 * NT) == 0:
                        pe.wait_ge(s["rows_filled"], 1 + 16 * (N_ROWS * i + ROWS0[1] + g + 1))
                else:
                    g, k, pair = n // 2, 0, n % 2
                    if n == 0:
                        pe.wait_ge(s["rows_filled"], 1 + 16 * (N_ROWS * i + ROWS0[a] + 1))
                m = P if a == 1 else SC
                for c in range(2):
                    h = g * HG + 2 * pair + c
                    dst = ex[e % 2][0:m, c, :]
                    if a == 0:
                        nc.tensor.matmul(dst, identb[0:SC, 0:SC], maskT[:], start=True, stop=False,
                                         skip_group_check=True)
                    ins = nc.tensor.matmul(dst, kst[a][0:rows, h, k * P:k * P + m], qst[a][0:rows, h, :],
                                           start=a != 0, stop=True, skip_group_check=a != 1)
                    if a == 2:
                        for part in range(3):
                            ins = nc.tensor.matmul(dst[:, S - CORNER:S], slopes[:, part, h, :],
                                                   corner[:, P - CORNER:P], start=False, stop=True,
                                                   skip_group_check=True)
                ins.then_inc(s["scores"], 1)

            def pv_step(i, a, n):
                e = PV0[a] + n
                pe.wait_ge(s["probs_ready"], 1 + N_EXP * i + 2 * e + 2)
                k = n % NT if a == 1 else 0
                g = n // NT if a == 1 else n
                if k == 0:
                    pe.wait_ge(s["strips_ready"], 1 + 3 * G * i + G * a + g)
                m = P if a == 1 else SC
                for c in range(HG):
                    tile = (2 * e + c // 2) % 4
                    ins = nc.tensor.matmul(pv[32 * c:32 * c + 32, 0, :], vx[a][:, k, g * HG + c, :],
                                           probs[0:m, tile, c % 2, :], start=k == 0,
                                           stop=(k == NT - 1 or a != 1))
                ins.then_inc(s["pv_done"], 1)

            def attention(i, a):
                pe.wait_ge(s["q_filled"], 1 + 16 * 9 * (3 * i + a + 1))
                if a == 1:
                    pe.wait_ge(s["k_filled"], 1 + 16 * 9 * (i + 1))
                    pe.wait_ge(s["v_ready"], 1 + i + 1)
                    pe.wait_ge(s["k_parts"], 1 + i + 1)
                else:
                    pe.wait_ge(s["kctx_filled"], 1 + 16 * 18 * (i + 1))
                    pe.wait_ge(s["vctx_ready"], 1 + i + 1)
                for kind, n in PLANS[a]:
                    if kind == "max":
                        max_tile(i, a, n)
                    elif kind == "rows":
                        nh = HG if a == 1 else H
                        e = N_ROWS * i + ROWS0[a] + n
                        pe.wait_ge(s["max_parts"], 1 + e + 1)
                        pe.wait_ge(s["rows_ready"], 1 + e)
                        done = sum(1 for q, m in PLANS[a][:PLANS[a].index(("rows", n))] if q == "heads")
                        pe.wait_ge(s["heads_ready"], 1 + 3 * G * i + G * a + done)
                        for k in range(NT):
                            cols = negp[:, k].rearrange("p a h -> p (a h)")
                            for r0 in range(0, 3 * nh, 32):
                                r1 = min(3 * nh, r0 + 32)
                                ins = nc.tensor.transpose(misc_b[r0:r1, k * P:(k + 1) * P], cols[:, r0:r1], identb[:])
                        ins.then_inc(s["rows_psum"], 1)
                    elif kind == "exp":
                        exp_tile(i, a, n)
                    elif kind == "pv":
                        pv_step(i, a, n)
                    elif kind == "heads":
                        e = 3 * G * i + G * a + n
                        pe.wait_ge(s["strips_ready"], 1 + e + 1)
                        pe.wait_ge(s["heads_ready"], 1 + e)
                        done = sum(1 for q, m in PLANS[a][:PLANS[a].index(("heads", n))] if q == "rows")
                        pe.wait_ge(s["rows_ready"], 1 + N_ROWS * i + ROWS0[a] + done)
                        for k in range(NT):
                            ins = nc.tensor.transpose(misc[:, 0, k * P:(k + 1) * P], strips[:, k * P:(k + 1) * P],
                                                      ident[:])
                        ins.then_inc(s["heads_psum"], 1)
                pe.wait_ge(s["heads_ready"], 1 + 3 * G * i + G * (a + 1))
                for k in range(NT):
                    ins = nc.tensor.transpose(misc[:, 0, k * P:(k + 1) * P], o[:, k, :], ident[:])
                ins.then_inc(s["oT_psum"], 1)
                pe.wait_ge(s["oT_ready"], 1 + 3 * i + a + 1)
                for k in range(NT):
                    ins = nc.tensor.matmul(mx[0][:, 0, k * P:(k + 1) * P], oT[:, k * P:(k + 1) * P], W[f"o{a}"],
                                           start=True, stop=True, skip_group_check=True)
                ins.then_inc(s["attn_psum"], 1)

            def down(mid_of, weights, dst, fs, sig):
                for f in fs:
                    for k in range(NT):
                        ins = nc.tensor.matmul(dst[:, k * P:(k + 1) * P], mid_of[:, f, k * P:(k + 1) * P],
                                               weights[:, f, :], start=(f == 0 and k == 0), stop=(f == NF - 1),
                                               skip_group_check=True)
                if sig:
                    ins.then_inc(sig, 1)

            with pe.Fori(0, B) as i:
                pe.wait_ge(s["ctx_loaded"], 1 + 16 * i + 16)
                nc.tensor.transpose(misc[:, 0, 0:SC], ctx_in[:], ident[0:SC, 0:SC]).then_inc(s["ctxT_psum"], 1)
                pe.wait_ge(s["ctxT_ready"], 1 + i + 1)
                for layer, a in enumerate((0, 2)):
                    nc.tensor.matmul(mx[0][:, 0, layer * SC:(layer + 1) * SC], W[f"k{a}"], ctxT[:],
                                     start=True, stop=True, skip_group_check=True)
                for layer, a in enumerate((0, 2)):
                    ins = nc.tensor.matmul(mx[1][0:SC, 0, layer * D:(layer + 1) * D], ctxT[:], W[f"v{a}"],
                                           start=True, stop=True, skip_group_check=True)
                ins.then_inc(s["kvctx_psum"], 1)
                pe.wait_ge(s["mask_num"], 1 + i + 1)
                for k in range(NT):
                    ins = nc.tensor.transpose(misc_b[0:SC, k * P:(k + 1) * P], mask_neg[:, k, :], identb[:])
                ins.then_inc(s["maskT_psum"], 1)
                pe.wait_ge(s["maskT_ready"], 1 + i + 1)
                transposes(i, 0, 0)
                pe.wait_ge(s["vctx_ready"], 1 + i + 1)
                project(i, 0)
                attention(i, 0)
                transposes(i, 1, 0)
                pe.wait_ge(s["attn_ready"], 1 + 3 * i + 1)
                project(i, 1)
                attention(i, 1)

                transposes(i, 2, 0)
                pe.wait_ge(s["zT_ready"], 1 + 5 * i + 3)
                for k in range(NT):
                    ins = nc.tensor.matmul(misc[:, 0, k * NE:(k + 1) * NE], zT[:, k * P:(k + 1) * P], gate_w[:],
                                           start=True, stop=True, skip_group_check=True)
                ins.then_inc(s["logit_psum"], 1)

                def pick_bias():
                    pe.wait_ge(s["hot_ready"], 1 + i + 1)
                    for k in range(NT):
                        ins = nc.tensor.transpose(pv[0:NE, 0, k * P:(k + 1) * P], hot[:, k, :], ident[:])
                    ins.then_inc(s["hotT_psum"], 1)
                    pe.wait_ge(s["hotT_ready"], 1 + i + 1)
                    for k in range(NT):
                        ins = nc.tensor.matmul(misc[:, 0, k * P:(k + 1) * P], hotT[:, k * P:(k + 1) * P], b2[:],
                                               start=True, stop=True, skip_group_check=True)
                    ins.then_inc(s["b2_psum"], 1)

                def up(e):
                    for half in range(2):
                        if e:
                            pe.wait_ge(s[["mid_act", "mid_dve"][half]], 1 + NE * i + e)
                        for f in range(2):
                            col = (2 * half + f) * P
                            ins = nc.tensor.matmul(ex[half][:, f, :], w1[:, e, col:col + P], zT[:],
                                                   start=True, stop=True)
                        ins.then_inc(s["up"], 1)

                pick_bias()
                up(0)
                for e in range(NE):
                    if e + 1 < NE:
                        up(e + 1)
                    pe.wait_ge(s["down_used"], 1 + NE * i + max(e - 1, 0))
                    pe.wait_ge(s["mid_act"], 1 + NE * i + e + 1)
                    down(mid[:, e % 2], w2[:, e], mx[e % 2][:, 0, :], (0, 1), None)
                    pe.wait_ge(s["mid_dve"], 1 + NE * i + e + 1)
                    down(mid[:, e % 2], w2[:, e], mx[e % 2][:, 0, :], (2, 3), s["down"])

                transposes(i, 3, 0)
                project(i, 2)
                attention(i, 2)

                transposes(i, 4, 0)
                pe.wait_ge(s["score_ready"], 1 + i + 1)
                for k in range(NT):
                    ins = nc.tensor.transpose(pv[:, 0, k * P:(k + 1) * P], score[:, k:k + 1].to_broadcast([P, P]),
                                              ident[:])
                ins.then_inc(s["rowscore_psum"], 1)
                pe.wait_ge(s["zT_ready"], 1 + 5 * i + 5)
                for f in range(NF):
                    nc.tensor.matmul(ex[f // 2][:, f % 2, :], fw1[:, f * P:(f + 1) * P], zT[:],
                                     start=True, stop=True).then_inc(s["fup"], 1)
                pe.wait_ge(s["attn_ready"], 1 + 3 * i + 3)
                for f in range(NF):
                    pe.wait_ge(s["fmid"], 1 + NF * i + f + 1)
                    down(mid[:, 0], fw2, mx[1][:, 0, :], (f,), s["fdown"] if f == NF - 1 else None)

        @block.vector
        def _(dve):
            start_at_one(dve, "vector")
            dve.wait_ge(s["consts"], 16 * N_CONST)
            dve.wait_ge(s["padded"], 3)
            chain = [0]
            CHAIN = 97

            def link(i, ins):
                chain[0] += 1
                ins.then_inc(s["dve_chain"], 1)
                dve.wait_ge(s["dve_chain"], 1 + CHAIN * i + chain[0])

            def layernorm(i, n, x, dst):
                for k in range(NT):
                    ins = nc.vector.bn_stats(stats[:, k, :], x[:, k, :])
                link(i, ins)
                nc.vector.memset(vareps[:, 0:1], 0.0)
                for k in range(NT):
                    ins = nc.vector.bn_aggr(meanvar[:, k, :], stats[:, k, :])
                link(i, ins)
                nc.vector.tensor_scalar(vareps[:], meanvar[:, :, 1], EPS, None, ALU.add).then_inc(s["var_ready"], 1)
                dve.wait_ge(s["rstd_ready"], 1 + LN * i + n + 1)
                for k in range(NT):
                    ins = nc.vector.tensor_scalar(dst[:, k, :], x[:, k, :], meanvar[:, k, 0:1], rstd[:, k:k + 1],
                                                  ALU.subtract, ALU.mult)
                ins.then_inc(s["z_ready"], 1)

            def split(i, parts, src, rest):
                link(i, nc.vector.tensor_copy(parts(0), src))
                link(i, nc.vector.tensor_tensor(rest, src, parts(0), ALU.subtract))
                link(i, nc.vector.tensor_copy(parts(1), rest))
                return nc.vector.tensor_tensor(parts(2), rest, parts(1), ALU.subtract)

            def projections(i, a):
                dve.wait_ge(s["q_psum"], 1 + 3 * i + a + 1)
                link(i, nc.vector.tensor_scalar(qf[:], mx[0][:, 0, :], C[f"bq{a}"], QSCALE, ALU.add, ALU.mult))
                dve.wait_ge(s["q_filled"], 1 + 16 * 9 * (3 * i + a))
                split(i, lambda p3: qp[:, p3, :], qf[:], qr[:]).then_inc(s["q_parts"], 1)
                if a == 1:
                    dve.wait_ge(s["k_psum"], 1 + i + 1)
                    link(i, nc.vector.tensor_scalar(kf[:], mx[1][:, 0, :], C["bk1"], None, ALU.add))
                    dve.wait_ge(s["k_filled"], 1 + 16 * 9 * i)
                    split(i, lambda p3: kp[:, p3, :], kf[:], kr[:]).then_inc(s["k_parts"], 1)
                    dve.wait_ge(s["v_psum"], 1 + i + 1)
                    for k in range(NT):
                        ins = nc.vector.tensor_tensor(vx[1][:, k, :, 0:DK],
                                                      pv[:, 0, k * P:(k + 1) * P].rearrange("p (h d) -> p h d", d=DK),
                                                      R["bv1"].rearrange("p (h d) -> p h d", d=DK), ALU.add)
                    ins.then_inc(s["v_ready"], 1)

            def attention(i, a):
                for kind, n in PLANS[a]:
                    if kind == "max":
                        e = MAX0[a] + n
                        dve.wait_ge(s["max_scores"], 1 + N_MAX * i + e + 1)
                        if a == 1:
                            h, k = divmod(n, NT)
                            if n % (HG * NT) == 0:
                                dve.wait_ge(s["max_parts"], 1 + N_ROWS * i + ROWS0[1] + h // HG)
                            nc.vector.tensor_reduce(negmax[:, k, h % HG:h % HG + 1], mx[e % 2][:, 0, :], AX.X, ALU.max,
                                                    negate=True).then_inc(s["max_taken"], 1)
                        else:
                            g, k = divmod(n, NT)
                            nc.vector.tensor_reduce(negmax[:, k, g * HG:(g + 1) * HG],
                                                    mx[e % 2][:, 0, 0:HG * SC].rearrange("p (h k) -> p h k", k=SC),
                                                    AX.X, ALU.max, negate=True).then_inc(s["max_taken"], 1)
                    elif kind == "parts":
                        nh = HG if a == 1 else H
                        e = N_ROWS * i + ROWS0[a] + n
                        dve.wait_ge(s["max_taken"], 1 + N_MAX * i + MAX0[a] + (HG * NT * (n + 1) if a == 1 else G * NT))
                        dve.wait_ge(s["rows_psum"], 1 + e)
                        parts = negp[:].rearrange("p k a h -> p k (a h)")[:, :, 0:3 * nh]\
                            .rearrange("p k (a h) -> p k a h", a=3)
                        split(i, lambda p3: parts[:, :, p3, :], negmax[:, :, 0:nh], negrest[:, :, 0:nh])\
                            .then_inc(s["max_parts"], 1)
                    elif kind == "heads":
                        e = 3 * G * i + G * a + n
                        dve.wait_ge(s["heads_psum"], 1 + e + 1)
                        view = misc[:, 0, :].rearrange("p (t c j) -> p t c j", t=NT, j=32)
                        link(i, nc.vector.reciprocal(rden[:], view[:, :, :, DK]))
                        nc.vector.tensor_tensor(
                            o[:].rearrange("p t (g c d) -> p t g c d", g=G, d=DK)[:, :, n],
                            view[:, :, :, 0:DK], rden[:].unsqueeze(3).to_broadcast([P, NT, HG, DK]), ALU.mult)\
                            .then_inc(s["heads_ready"], 1)

            def add_residual(i, a, dst):
                dve.wait_ge(s["attn_psum"], 1 + 3 * i + a + 1)
                dve.wait_ge(s["res_ready"], 1 + 3 * i + a + 1)
                ins = nc.vector.tensor_tensor(dst[:], mx[0][:, 0, :].rearrange("p (t d) -> p t d", d=D), res[:],
                                              ALU.add)
                ins.then_inc(s["attn_ready"], 1)
                dve.wait_ge(s["attn_ready"], 1 + 3 * i + a + 1)

            with dve.Fori(0, B) as i:
                dve.wait_ge(s["mask_loaded"], 1 + 16 * i + 16)
                dve.wait_ge(s["maskT_psum"], 1 + i)
                nc.vector.tensor_scalar(mask_neg[:], mask_in[:], 0, -BIG, ALU.is_equal, ALU.mult)\
                    .then_inc(s["mask_num"], 1)
                dve.wait_ge(s["kvctx_psum"], 1 + i + 1)
                for layer, a in enumerate((0, 2)):
                    ins = nc.vector.tensor_scalar(kc[:, layer], mx[0][:, 0, layer * SC:(layer + 1) * SC],
                                                  C[f"bk{a}"], None, ALU.add)
                link(i, ins)
                dve.wait_ge(s["kctx_filled"], 1 + 16 * 18 * i)
                split(i, lambda p3: kcp[:, p3], kc[:], kcr[:]).then_inc(s["kctx_parts"], 1)
                for layer, a in enumerate((0, 2)):
                    ins = nc.vector.tensor_tensor(
                        vx[a][:, 0, :, 0:DK],
                        mx[1][0:SC, 0, layer * D:(layer + 1) * D].rearrange("p (h d) -> p h d", d=DK),
                        R[f"bv{a}"][0:SC].rearrange("p (h d) -> p h d", d=DK), ALU.add)
                ins.then_inc(s["vctx_ready"], 1)

                dve.wait_ge(s["x_loaded"], 1 + 16 * i + 16)
                layernorm(i, 0, x0, z[:, 0])
                projections(i, 0)
                attention(i, 0)
                add_residual(i, 0, x1)
                layernorm(i, 1, x1, z[:, 1])
                dve.wait_ge(s["z_ready"], 1 + LN * i + 2)
                layernorm(i, 2, z[:, 1], z[:, 0])
                projections(i, 1)
                attention(i, 1)
                add_residual(i, 1, y)
                layernorm(i, 3, y, z[:, 0])

                dve.wait_ge(s["logit_psum"], 1 + i + 1)
                link(i, nc.vector.tensor_tensor(logit[:], misc[:, 0, 0:NT * NE].rearrange("p (t e) -> p t e", e=NE),
                                                gate_b[:].unsqueeze(1).to_broadcast([P, NT, NE]), ALU.add))
                link(i, nc.vector.tensor_reduce(top[:], logit[:], AX.X, ALU.max))
                link(i, nc.vector.tensor_tensor(pick[:], logit[:], top[:].unsqueeze(2).to_broadcast([P, NT, NE]),
                                                ALU.is_equal))
                link(i, nc.vector.tensor_tensor(pick[:], pick[:], falling[:].unsqueeze(1).to_broadcast([P, NT, NE]),
                                                ALU.mult))
                link(i, nc.vector.tensor_reduce(top[:], pick[:], AX.X, ALU.max))
                nc.vector.tensor_tensor(hot[:], falling[:].unsqueeze(1).to_broadcast([P, NT, NE]),
                                        top[:].unsqueeze(2).to_broadcast([P, NT, NE]), ALU.is_equal)\
                    .then_inc(s["hot_ready"], 1)
                link(i, nc.vector.tensor_tensor(x1[:], x1[:], y[:], ALU.add))
                dve.wait_ge(s["b2_psum"], 1 + i + 1)
                nc.vector.tensor_tensor(x2[:], x1[:], misc[:, 0, :].rearrange("p (t d) -> p t d", d=D), ALU.add)\
                    .then_inc(s["acc_ready"], 1)

                def relu_half(e):
                    dve.wait_ge(s["up"], 1 + 2 * NE * i + 2 * e + 2)
                    dve.wait_ge(s["down"], 1 + NE * i + max(e - 1, 0))
                    for f in range(2, NF):
                        ins = nc.vector.tensor_scalar(mid[:, e % 2, f], ex[1][:, f - 2], b1[:, e, f:f + 1], 0.0,
                                                      ALU.add, ALU.max)
                    ins.then_inc(s["mid_dve"], 1)

                relu_half(0)
                for e in range(NE):
                    if e + 1 < NE:
                        relu_half(e + 1)
                    dve.wait_ge(s["down"], 1 + NE * i + e + 1)
                    dve.wait_ge(s["acc_ready"], 1 + i + 1)
                    dve.wait_ge(s["down_used"], 1 + NE * i + e)
                    for k in range(NT):
                        ins = nc.vector.scalar_tensor_tensor(
                            out=x2[:, k, :], in0=mx[e % 2][:, 0, k * P:(k + 1) * P], scalar=hot[:, k, e:e + 1],
                            in1=x2[:, k, :], op0=ALU.mult, op1=ALU.add)
                    ins.then_inc(s["down_used"], 1)
                dve.wait_ge(s["down_used"], 1 + NE * i + NE)

                layernorm(i, 4, x2, z[:, 0])
                projections(i, 2)
                attention(i, 2)
                add_residual(i, 2, x3)
                layernorm(i, 5, x3, z[:, 0])
                dve.wait_ge(s["z_ready"], 1 + LN * i + 6)

                for k in range(NT):
                    link(i, nc.vector.tensor_tensor(junk[:, 0:D], z[:, 0, k, :], R["router"], ALU.mult))
                    ins = nc.vector.tensor_reduce(score[:, k:k + 1], junk[:, 0:D], AX.X, ALU.add)
                    if k + 1 < NT:
                        link(i, ins)
                ins.then_inc(s["score_ready"], 1)
                link(i, nc.vector.memset(counts[:], 0.0))
                dve.wait_ge(s["rowscore_psum"], 1 + i + 1)
                dve.wait_ge(s["score_ready"], 1 + i + 1)
                for k in range(NT):
                    all_scores, own = pv[:, 0, :], score[:, k:k + 1]
                    if k:
                        link(i, nc.vector.tensor_scalar(junk[:, 0:k * P], all_scores[:, 0:k * P], own, None,
                                                        ALU.is_ge, ALU.add, accum_out=counts[:, k, 0:1]))
                    link(i, nc.vector.tensor_scalar(junk[:, k * P:S], all_scores[:, k * P:S], own, None,
                                                    ALU.is_gt, ALU.add, accum_out=counts[:, k, 1:2]))
                    link(i, nc.vector.scalar_tensor_tensor(out=junk[:, 0:P], in0=all_scores[:, k * P:(k + 1) * P],
                                                           scalar=own, in1=lower[:], op0=ALU.is_equal, op1=ALU.mult))
                    link(i, nc.vector.tensor_reduce(counts[:, k, 2:3], junk[:, 0:P], AX.X, ALU.add))
                link(i, nc.vector.tensor_reduce(rank[:], counts[:], AX.X, ALU.add))
                dve.wait_ge(s["sig_ready"], 1 + i + 1)
                link(i, nc.vector.tensor_scalar(esig[:], esig[:], 1.0, None, ALU.add))
                link(i, nc.vector.reciprocal(weight[:], esig[:]))
                link(i, nc.vector.scalar_tensor_tensor(out=weight[:], in0=rank[:], scalar=float(TOPK) - 0.5,
                                                       in1=weight[:], op0=ALU.is_lt, op1=ALU.mult))
                link(i, nc.vector.tensor_tensor(x3[:], x3[:], z[:, 0], ALU.add))
                dve.wait_ge(s["fdown"], 1 + i + 1)
                link(i, nc.vector.tensor_tensor(junk[:].rearrange("p (t d) -> p t d", d=D),
                                                mx[1][:, 0, :].rearrange("p (t d) -> p t d", d=D),
                                                R["fb2"].unsqueeze(1).to_broadcast([P, NT, D]), ALU.add))
                dve.wait_ge(s["stored"], 1 + 16 * i)
                for k in range(NT):
                    nc.vector.scalar_tensor_tensor(
                        out=out_sb[:, k, :], in0=junk[:, k * P:(k + 1) * P], scalar=weight[:, k:k + 1],
                        in1=x3[:, k, :], op0=ALU.mult, op1=ALU.add).then_inc(s["out_ready"], 1)
                assert chain[0] == CHAIN


def shape_constants():
    import numpy as np

    bf = np.dtype("bfloat16")

    def parts(a):
        out, rest = [], a.astype(np.float32)
        for _ in range(3):
            p = rest.astype(bf)
            out.append(p)
            rest = rest - p.astype(np.float32)
        return out

    slope = np.array([2.0 ** (-8.0 * (h + 1) / H) for h in range(H)], np.float32)
    eye = np.eye(SC, dtype=np.float32)
    keys, toks = np.arange(SC, dtype=np.float32), np.arange(S, dtype=np.float32)
    k_lin = parts(-slope[:, None] * (keys + (S - SC))[None, :])
    q_lin = parts(slope[:, None] * toks[None, :])
    one_k, one_q = np.ones((H, SC), bf), np.ones((H, S), bf)
    toks3 = toks[S - P:]
    return {
        "ident": np.eye(P, dtype=np.float32),
        "identb": np.eye(P).astype(bf),
        "eye4": np.ascontiguousarray(np.repeat(eye[:, None, :], HG, 1)).astype(bf),
        "slopes": np.stack([(eye[:, None, :] * p.astype(np.float32)[None, :, None]).astype(bf)
                            for p in parts(-2 * slope)], 1),
        "corner": np.maximum(0, toks3[None, :] - keys[:, None] - (S - SC)).astype(bf),
        "lower": (np.arange(P)[None, :] < np.arange(P)[:, None]).astype(np.float32),
        "falling": np.tile(np.arange(NE, 0, -1).astype(np.float32), (P, 1)),
        "halfneg": np.full((P, NT), -0.5, np.float32),
        "kones": np.ones((3, H, S), bf),
        "kzeros": np.zeros((ALIBI, H, SC), bf),
        "kalibi": np.stack(k_lin + [one_k] * 3),
        "qalibi": np.stack([one_q] * 3 + q_lin),
    }


def kernel(**inputs):
    import numpy as np
    import concourse.bacc as bacc
    from concourse.bass_utils import run_bass_kernel_spmd

    a = {k: np.asarray(v) for k, v in inputs.items()}
    dh = np.arange(D).reshape(H, DK).T.reshape(-1)
    x0, f0, x1, f1 = "L0_xattn_", "L0_ffn_", "L1_xattn_", "L1_ffn_"
    wkv, bkv = a[x1 + "Wkv"], a[x1 + "bkv"]
    w = [a[x0 + "W_q"].T[:, dh], a[x0 + "W_k"].T[:, dh], a[x0 + "W_v"].T, a[x0 + "W_o"].T,
         a[f0 + "wq"][:, dh], a[f0 + "wk"][:, dh], a[f0 + "wv"], a[f0 + "wo"],
         a[x1 + "Wq"][:, dh], wkv[:, :D][:, dh], wkv[:, D:], a[x1 + "Wo"]]
    c = [a[x0 + "b_q"][dh], a[x0 + "b_k"][dh], a[f0 + "bq"][dh], a[f0 + "bk"][dh], a[x1 + "bq"][dh], bkv[:D][dh],
         a[f0 + "ln1_g"], a[f0 + "ln1_b"], a[f0 + "ln2_g"], a[f0 + "ln2_b"]]
    r = [a[x0 + "b_v"], a[x0 + "b_o"], a[f0 + "bv"], a[f0 + "bo"], bkv[D:], a[x1 + "bo"], a[f1 + "b2"],
         a[f1 + "w_router"]]
    arrays = {
        "x": a["x"], "ctx": a["ctx_1024"], "mask": a["mask_Bx1xSxS2_ik1"],
        "w": np.stack(w, 1), "c": np.stack(c, 1), "r": np.stack(r, 0),
        "gate_w": a[f0 + "gate_w"], "gate_b": a[f0 + "gate_b"],
        "w1": a[f0 + "w1"].transpose(1, 0, 2),
        "b1": a[f0 + "b1"].reshape(NE, NF, P).transpose(2, 0, 1),
        "w2": a[f0 + "w2"].reshape(NE, NF, P, D).transpose(2, 0, 1, 3),
        "b2": a[f0 + "b2"],
        "fw1": a[f1 + "W1"], "fb1": a[f1 + "b1"].reshape(NF, P).T,
        "fw2": a[f1 + "W2"].reshape(NF, P, D).transpose(1, 0, 2),
    }
    arrays.update(shape_constants())
    arrays = {k: np.ascontiguousarray(v) for k, v in arrays.items()}
    nc = bacc.Bacc("TRN2", target_bir_lowering=False, num_devices=1)
    tensors = {k: nc.dram_tensor(f"in_{k}", v.shape, mybir.dt.from_np(v.dtype), kind="ExternalInput").ap()
               for k, v in arrays.items()}
    tensors["out"] = nc.dram_tensor("out_dram", (B, S, D), F32, kind="ExternalOutput").ap()
    build(nc, tensors)
    result = run_bass_kernel_spmd(nc, [{f"in_{k}": v for k, v in arrays.items()}], core_ids=[0])
    return result.results[0]["out_dram"]
```

```python
from contextlib import ExitStack

import concourse.bass as bass
from concourse import mybir

F32 = mybir.dt.float32
BF16 = mybir.dt.bfloat16
I32 = mybir.dt.int32
ALU = mybir.AluOpType
ACT = mybir.ActivationFunctionType
AX = mybir.AxisListType

B, S, D, SC = 4, 512, 128, 77
H = 16
DK = D // H
P = 128
NT = S // P
G, HG = 4, 4
NE, F = 8, 512
NF = F // P
TOPK = S // 2
EPS = 1e-5
PROD = 9 * DK
ALIBI = 6
CORNER = S - (S - SC) - 1
BIG = 2.0 ** 60
QSCALE = DK ** -0.5
MAXROW = P - 3
SCP = 96

W_NAMES = ["q0", "k0", "v0", "o0", "q1", "k1", "v1", "o1", "q2", "k2", "v2", "o2"]
C_NAMES = ["bq0", "bk0", "bq1", "bk1", "bq2", "bk2", "g1", "c1", "g2", "c2"]
R_NAMES = ["bv0", "bo0", "bv1", "bo1", "bv2", "bo2", "fb2", "router"]

RING = 3
NPROBS = [6, 6]
LEAD = 12

KINDS = {
    "load": (None, [("sp", 0.1)], []),
    "ctx": ("act_took", [("pe", 0.2), ("act", 0.3)], []),
    "mask": ("act_took", [("dve", 0.4), ("pe", 0.4), ("act", 0.5)], []),
    "z": ("act_took", [("pe", 0.9), ("act", 0.5)], ["norm"]),
    "q": ("act_took", [("pe", 1.0), ("act", 0.5)], ["z"]),
    "k": ("act_took", [("pe", 1.0), ("act", 0.5)], ["z"]),
    "rows": ("act_took", [("pe", 0.5), ("act", 0.5), ("dma", 2.5)], ["parts"]),
    "o": ("act_took", [("pe", 0.9), ("act", 0.5)], ["heads"]),
    "hot": ("act_took", [("pe", 0.5), ("act", 0.5)], ["logit"]),
    "ctxkv": ("dve_took", [("pe", 0.4), ("dve", 0.4)], ["ctx"]),
    "v": ("dve_took", [("pe", 0.9), ("dve", 0.9)], ["z"]),
    "heads": ("dve_took", [("pe", 0.9), ("dve", 0.5)], ["strips"]),
    "attn": ("dve_took", [("pe", 0.9), ("dve", 0.6)], ["o"]),
    "logit": ("dve_took", [("pe", 0.4), ("dve", 1.0)], ["z"]),
    "bias": ("dve_took", [("pe", 0.4), ("dve", 0.6)], ["hot"]),
    "rank": ("dve_took", [("pe", 0.9), ("dve", 6.0)], ["score"]),
    "max": ("max_taken", [("pe", 0.25), ("dve", 0.6)], ["split", "ctxsplit"]),
    "exp": ("probs", [("pe", 0.25), ("act", 0.48)], ["rows"]),
    "up": ("mid", [("pe", 0.9), ("act", 0.6)], ["z"]),
    "fup": ("mid", [("pe", 0.9), ("act", 0.9)], ["z"]),
    "split": (None, [("dve", 2.2), ("dma", 8.0)], ["q", "k"]),
    "ctxsplit": (None, [("dve", 0.8), ("dma", 8.0)], ["ctxkv"]),
    "parts": (None, [("dve", 0.6)], ["max"]),
    "pv": (None, [("pe", 0.8)], ["exp"]),
    "strips": (None, [("act", 0.5)], ["pv"]),
    "stats": (None, [("dve", 1.9), ("pool", 1.0)], ["attn", "acc", "norm"]),
    "norm": (None, [("dve", 0.9)], ["stats"]),
    "residual": (None, [("pool", 1.0)], []),
    "base": (None, [("dve", 0.6)], []),
    "down": (None, [("pe", 0.9)], ["up", "fup"]),
    "acc": (None, [("dve", 1.0)], ["down"]),
    "score": (None, [("dve", 2.0)], ["norm"]),
    "sigmoid": (None, [("act", 0.2)], ["score"]),
    "sum": (None, [("dve", 1.2)], ["down", "score"]),
    "out": (None, [("dve", 1.1)], ["sum"]),
}
AHEAD = 3
CONTEXT_TIMES = {
    ("max", 0): [("pe", 0.5), ("dve", 0.4)], ("max", 2): [("pe", 0.4), ("dve", 0.4)],
    ("exp", 0): [("pe", 0.4), ("act", 0.48)], ("exp", 2): [("pe", 0.4), ("act", 0.48)],
    ("parts", 0): [("dve", 1.2)], ("parts", 2): [("dve", 1.2)],
}
HOP = 0.2
BIAS = [2.0, 2.0]
USES_RING = {k for k, kind in KINDS.items() if kind[0]}


class Step:

    def __init__(self, st, kind, a=0, x=0):
        self.st, self.kind, self.a, self.x = st, kind, a, x
        self.n, self.bank, self.freed = 0, None, None


def attention_steps(st, a):
    steps, groups = [], G
    per = HG * NT if a == 1 else NT
    exps = HG * NT if a == 1 else HG
    emitted = 0

    def add(kind, x=0):
        steps.append(Step(st, kind, a, x))

    def take(n):
        nonlocal emitted
        for _ in range(n):
            if emitted < groups * per:
                add("max", emitted)
            emitted += 1
            if a == 1:
                if emitted % per == 0 and emitted <= groups * per:
                    add("parts", emitted // per - 1)
                if emitted % per == 3 and per < emitted < (groups + 1) * per:
                    add("rows", emitted // per - 1)
    if a == 1:
        take(per + LEAD)
    else:
        take(groups * per)
        add("parts")
        add("rows")
    total = groups * exps
    for e in range(total + 12):
        if e < total:
            add("exp", e)
            if a == 1:
                take(1)
        late = HG + 2 if a == 1 else 0
        if e >= exps + 5 + late and (e - exps - 5 - late) % exps == 0 and (e - exps - 5 - late) // exps < groups:
            add("heads", (e - exps - 5 - late) // exps)
        if e >= 5 and (e - 5) % HG == 0 and (e - 5) // HG < total // HG:
            k = (e - 5) // HG
            add("pv", k)
            if (k + 1) % (exps // HG) == 0:
                add("strips", (k + 1) // (exps // HG) - 1)
    have = {s.x for s in steps if s.kind == "heads"}
    for g in range(groups):
        if g not in have:
            add("heads", g)
    add("o")
    add("attn")
    return steps


def stream_steps(st):
    steps = []

    def add(kind, a=0, x=0):
        steps.append(Step(st, kind, a, x))

    if st == 0:
        add("ctx")
        add("mask")
        add("ctxkv")
        add("stats", 0)
        add("ctxsplit")
        add("norm", 0)
        add("residual", 0)
        add("z", 0)
        add("q", 0)
        add("split", 0, 0)
        add("load")
        steps += attention_steps(0, 0)
        add("stats", 1)
        add("norm", 1)
        add("stats", 2)
        add("residual", 1)
        add("norm", 2)
        add("z", 1)
        add("q", 1)
        add("k", 1)
        add("v", 1)
        add("split", 1, 0)
        add("split", 1, 1)
        steps += attention_steps(0, 1)
    else:
        add("stats", 0)
        add("base")
        add("norm", 0)
        add("z", 0)
        add("ctx")
        add("logit")
        tiles = [(e, f) for e in range(NE) for f in range(NF)]
        for n in range(AHEAD):
            add("up", 0, tiles[n])
        add("hot")
        add("ctxkv")
        add("bias")
        add("ctxsplit")
        add("load")
        for n, (e, f) in enumerate(tiles):
            if n + AHEAD < len(tiles):
                add("up", 0, tiles[n + AHEAD])
            add("down", 0, (e, f))
            if f == NF - 1:
                add("acc", 0, e)
        add("stats", 1)
        add("residual", 2)
        add("norm", 1)
        add("z", 2)
        add("q", 2)
        add("split", 2, 0)
        steps += attention_steps(1, 2)
        add("stats", 2)
        add("norm", 2)
        add("z", 3)
        add("score")
        for f in range(NF):
            add("fup", 0, f)
            if f == 1:
                add("rank")
        add("sigmoid")
        for f in range(NF):
            add("down", 1, (0, f))
        add("sum")
        add("out")
    seen = {}
    for s in steps:
        key = KINDS[s.kind][0] or s.kind
        s.n = seen.get(key, 0)
        seen[key] = s.n + 1
    ring = [s for s in steps if s.kind in USES_RING]
    for u, s in enumerate(ring):
        s.bank = u % RING
        if u >= RING:
            before = ring[u - RING]
            s.freed = (KINDS[before.kind][0], before.n + 1)
        else:
            before = [b for v, b in enumerate(ring) if v % RING == s.bank][-1]
            s.freed = (KINDS[before.kind][0], 0)
    return steps, seen


STEPS, TOTAL = zip(*[stream_steps(st) for st in range(2)])


def merged():
    free = {}
    done = [{}, {}]
    bank_free = [{}, {}]
    taken, order = [0, 0], []

    def start(q):
        seen = done[q.st]
        ready = [seen[k][-1] for k in KINDS[q.kind][2] if k in seen]
        if q.kind == "exp":
            ready = [seen["rows"][-1 if q.a != 1 else (0 if q.st else 1) + q.x // (HG * NT)]]
        elif q.kind == "pv":
            ready = [seen["exp"][HG * (q.n + 1) - 1]]
        elif q.kind == "down":
            ready = [(seen["up"] + seen.get("fup", []))[q.n]]
            if q.x[1] == 0 and q.x[0]:
                ready.append(seen["acc"][q.x[0] - 1])
        if q.bank is not None:
            ready.append(bank_free[q.st].get(q.bank, 0.0))
        return max([free.get(KINDS[q.kind][1][0][0], 0.0)] + [r + HOP for r in ready])

    while any(taken[st] < len(STEPS[st]) for st in range(2)):
        ways = [(start(q), BIAS[st] * taken[st] / len(STEPS[st]), st, q) for st in range(2)
                for q in STEPS[st][taken[st]:taken[st] + 1]]
        together = [way for way in ways if order and {order[-1].kind, way[3].kind} <= {"fup", "rank"}]
        when, _, st, q = min(together or ways, key=lambda way: (way[0] + way[1], way[2]))
        taken[st] += 1
        order.append(q)
        for k, (engine, us) in enumerate(CONTEXT_TIMES.get((q.kind, q.a), KINDS[q.kind][1])):
            when = when if engine == "dma" else max(when + HOP * (k > 0), free.get(engine, 0.0))
            when += us
            if engine != "dma":
                free[engine] = when
        done[st].setdefault(q.kind, []).append(when)
        if q.bank is not None:
            bank_free[st][q.bank] = when
    return order


def find(st, kind, a=None, x=None):
    return next(s for s in STEPS[st] if s.kind == kind and a in (None, s.a) and x in (None, s.x))


def build(nc, t):
    ctx = ExitStack()

    def sb(name, shape, dt=F32):
        return ctx.enter_context(nc.sbuf_tensor(name, shape, dt))

    def bank(name):
        return ctx.enter_context(nc.psum_tensor(name, [P, 512], F32))

    def sem(name):
        return ctx.enter_context(nc.semaphore(name))

    with ctx:
        w_sb = sb("w_sb", [P, len(W_NAMES), D])
        W = {n: w_sb[:, k, :] for k, n in enumerate(W_NAMES)}
        c_sb = sb("c_sb", [P, len(C_NAMES)])
        C = {n: c_sb[:, k:k + 1] for k, n in enumerate(C_NAMES)}
        qbias = sb("qbias", [P, 3])
        r_sb = sb("r_sb", [P, len(R_NAMES), D])
        R = {n: r_sb[:, k, :] for k, n in enumerate(R_NAMES)}
        gate_w = sb("gate_w", [P, NE])
        gate_b = sb("gate_b", [P, NE])
        w1 = sb("w1", [P, NE, F])
        b1 = sb("b1", [P, NE, NF])
        w2 = sb("w2", [P, NE, NF, D])
        b2 = sb("b2", [NE, D])
        fw1 = sb("fw1", [P, F])
        fb1 = sb("fb1", [P, NF])
        fw2 = sb("fw2", [P, NF, D])
        ident = sb("ident", [P, P])
        identb = sb("identb", [P, P], BF16)
        eye4 = sb("eye4", [SC, HG, SC], BF16)
        lower = sb("lower", [P, P])
        falling = sb("falling", [P, NE])
        halfneg = sb("halfneg", [P, NT])
        slopes = sb("slopes", [SC, 3, H, SC], BF16)
        corner = sb("corner", [SC, P], BF16)

        x0 = sb("x0", [P, NT, D])
        x1 = sb("x1", [P, NT, D])
        u1 = sb("u1", [P, NT, D])
        y = sb("y", [P, NT, D])
        x2 = sb("x2", [P, NT, D])
        x3 = sb("x3", [P, NT, D])
        mask_in = sb("mask_in", [P, NT, SC], I32)
        mask_neg = sb("mask_neg", [P, NT, SC], BF16)
        maskT = sb("maskT", [SCP, S], BF16)
        logit = sb("logit", [P, NT, NE])
        top = sb("top", [P, NT])
        hot = sb("hot", [P, NT, NE])
        pick = sb("pick", [P, NT, NE])
        hotT = sb("hotT", [NE, S])
        score = sb("score", [P, NT])
        junk = sb("junk", [P, S])
        counts = sb("counts", [P, NT, 3])
        rank = sb("rank", [P, NT])
        esig = sb("esig", [P, NT])
        weight = sb("weight", [P, NT])
        kp = sb("kp", [P, 3, S], BF16)
        qst01 = sb("qst01", [P, H, S], BF16)
        qst = [qst01, qst01, sb("qst2", [P, H, S], BF16)]
        kst = [sb("kst0", [P, H, SCP], BF16), sb("kst1", [P, H, S], BF16), sb("kst2", [P, H, SCP], BF16)]
        vx = [sb("vx0", [SCP, 1, H, 32]), sb("vx1", [P, NT, H, 32]), sb("vx2", [SCP, 1, H, 32])]

        class Stream:

            def __init__(self, st):
                def own(name, shape, dt=F32):
                    return sb(f"{name}_{st}", shape, dt)

                self.z = own("z", [P, NT, D])
                self.zT = own("zT", [P, S])
                self.res = own("res", [P, NT, D])
                self.stats = own("stats", [P, NT, 6])
                self.meanvar = own("meanvar", [P, NT, 2])
                self.vareps = own("vareps", [P, NT])
                self.rstd = own("rstd", [P, NT])
                self.lin = own("lin", [P, S])
                self.rest = own("rest", [P, S])
                self.qp = own("qp", [P, 3, S], BF16)
                self.ctx_in = own("ctx_in", [SC, D])
                self.ctxT = own("ctxT", [P, SC])
                self.kc = own("kc", [P, SC])
                self.kcr = own("kcr", [P, SC])
                self.kcp = own("kcp", [P, 3, SC], BF16)
                self.negmax = own("negmax", [P, NT, H])
                self.negrest = own("negrest", [P, NT, H])
                self.negp = own("negp", [P, NT, 3, H], BF16)
                self.mT = own("mT", [3 * H, S], BF16)
                self.probs = own("probs", [P, NPROBS[st], S])
                self.strips = self.lin
                self.rden = own("rden", [P, NT, HG])
                self.ring = [bank(f"ring{st}_{k}") for k in range(RING)]
                self.acc = bank(f"acc{st}")

        streams = [Stream(0), Stream(1)]
        mid = streams[1].probs

        counted = {
            "sync": "x_loaded ctx_loaded mask_loaded kctx_filled q_filled k_filled rows_filled stored",
            "tensor": "for_act for_dve max_scores scores for_mid pv_done down_done",
            "scalar": "act_took probs mid strips_ready sig_ready",
            "vector": "dve_took max_taken mask_num var_ready z_ready split_done kctx_parts kctx_lin max_parts "
                      "base_ready acc_done score_ready weight_ready summed out_ready",
            "gpsimd": "rstd_ready res_ready",
        }
        batch_counts = [{
            "x_loaded": 16 * (1 - st), "ctx_loaded": 16, "mask_loaded": 16 * (1 - st), "kctx_filled": 16 * 9,
            "stored": 16 * st, "q_filled": 16 * 9 * (2 - st), "k_filled": 16 * 9 * (1 - st),
            "rows_filled": 16 * sum(q.kind == "rows" for q in STEPS[st]),
            "for_act": TOTAL[st]["act_took"], "for_dve": TOTAL[st]["dve_took"], "max_scores": TOTAL[st]["max_taken"],
            "scores": TOTAL[st]["probs"], "for_mid": TOTAL[st].get("mid", 0), "pv_done": TOTAL[st]["pv"],
            "down_done": TOTAL[st].get("down", 0), "strips_ready": G * (2 - st), "sig_ready": st,
            "mask_num": 1 - st, "var_ready": 3, "z_ready": 3, "split_done": TOTAL[st]["split"], "kctx_parts": 1,
            "kctx_lin": 1, "max_parts": TOTAL[st]["parts"], "base_ready": st, "acc_done": NE * st,
            "score_ready": st, "weight_ready": st, "summed": st, "out_ready": st,
            "rstd_ready": 3, "res_ready": TOTAL[st]["residual"],
            "act_took": TOTAL[st]["act_took"], "dve_took": TOTAL[st]["dve_took"], "max_taken": TOTAL[st]["max_taken"],
            "probs": TOTAL[st]["probs"], "mid": TOTAL[st].get("mid", 0),
        } for st in range(2)]
        signals = [{n: sem(f"{n}_{st}") for names in counted.values() for n in names.split()} for st in range(2)]
        sig0, sig1 = signals
        per_batch = {signals[st][n]: count for st in range(2) for n, count in batch_counts[st].items()}
        consts, consts2, ones, ones1, cleared, cleared1, padded, pool_chain, qbias_ready, dma_order = (
            sem(n) for n in ("consts", "consts2", "ones", "ones1", "cleared", "cleared1", "padded", "pool_chain",
                             "qbias_ready", "dma_order"))
        chains = [sem(f"dve_chain{k}") for k in range(3)]

        def start_at_one(eng, name):
            for st in range(2):
                for n in counted[name].split():
                    eng.sem_inc(signals[st][n], 1)

        def counter(eng):
            def at(semaphore, b, count):
                per = per_batch[semaphore]
                if isinstance(b, int):
                    return per * b + (1 + count)
                value = eng.alloc_register()
                eng.reg_add(value, eng.to_reg(per * b), 1 + count)
                return value
            return at

        def run(eng, body):
            for q in STEPS[0]:
                body(0, q, 0)
            with eng.Fori(0, B - 1) as j:
                for q in merged():
                    body(j + 1 if q.st == 0 else j, q, 1)
            for q in STEPS[1]:
                body(B - 1, q, 2)

        N_CONST, N_CONST2 = 7, 16
        block = ctx.enter_context(nc.Block())

        @block.sync
        def _(sp):
            start_at_one(sp, "sync")

            def load(st, b):
                if st == 0:
                    sp.dma_start(x0[:], t["x"][bass.ds(b, 1)].rearrange("o (t p) d -> p (o t) d", p=P))\
                        .then_inc(sig0["x_loaded"], 16)
                sp.dma_start(streams[st].ctx_in[:], t["ctx"][bass.ds(b, 1)].rearrange("o k d -> (o k) d"))\
                    .then_inc(signals[st]["ctx_loaded"], 16)
                if st == 0:
                    sp.dma_start(mask_in[:], t["mask"][bass.ds(b, 1)].rearrange("o e (t p) k -> p (o e t) k", p=P))\
                        .then_inc(sig0["mask_loaded"], 16)

            def constants():
                for dst, name in [(ident, "ident"), (halfneg, "halfneg"), (c_sb, "c"), (w_sb, "w"),
                                  (identb, "identb"), (eye4, "eye4")]:
                    sp.dma_start(dst[:], t[name]).then_inc(consts, 16)
                sp.dma_start(r_sb[:], t["r"].partition_broadcast(P)).then_inc(consts, 16)
                sp.wait_ge(cleared, 3)
                sp.dma_start(kst[0][MAXROW:P, :, 0:SC], t["kones"][:, :, 0:SC]).then_inc(ones, 16)

            def constants_of_later_steps():
                sp.wait_ge(cleared1, 3)
                sp.dma_start(kst[1][MAXROW:P], t["kones"]).then_inc(ones1, 16)
                sp.dma_start(kst[2][PROD:PROD + ALIBI, :, 0:SC], t["kalibi"]).then_inc(consts2, 16)
                sp.dma_start(kst[2][MAXROW:P, :, 0:SC], t["kones"][:, :, 0:SC]).then_inc(consts2, 16)
                sp.dma_start(qst[2][PROD:PROD + ALIBI], t["qalibi"]).then_inc(consts2, 16)
                sp.dma_start(gate_b[:], t["gate_b"].partition_broadcast(P)).then_inc(consts2, 16)
                for dst, name in [(slopes, "slopes"), (corner, "corner"), (fb1, "fb1"), (b1, "b1"), (b2, "b2"),
                                  (gate_w, "gate_w"), (lower, "lower"), (falling, "falling"), (w1, "w1"), (w2, "w2"),
                                  (fw1, "fw1"), (fw2, "fw2")]:
                    sp.dma_start(dst[:], t[name]).then_inc(consts2, 16)

            def spread(dst, parts, width, filled, is_query):
                for i3 in range(3):
                    for j3 in range(3):
                        row = (i3 * 3 + j3) * DK
                        to = dst[row:row + DK, :, 0:width]
                        sp.dma_start(to.rearrange("d h t -> d (h t)") if width == S else to,
                                     parts[:, i3 if is_query else j3, :]).then_inc(filled, 16)

            at = counter(sp)

            def body(b, q, section):
                st, v, sig = q.st, streams[q.st], signals[q.st]
                if q.kind == "load":
                    if section < 2:
                        took = at(sig["for_act"], b, find(st, "ctx").n + 1)
                        if st == 0:
                            masked, added = at(sig0["mask_num"], b, 1), at(sig0["res_ready"], b, 1)
                            normed = at(sig0["z_ready"], b, 1)
                            sp.wait_ge(sig0["mask_num"], masked)
                            sp.wait_ge(sig0["res_ready"], added)
                            sp.wait_ge(sig0["z_ready"], normed)
                        sp.wait_ge(sig["for_act"], took)
                        sp.sem_inc(dma_order, 1)
                        load(st, (b + 1) % B if st == 0 else b + 1)
                elif q.kind == "ctxsplit":
                    sp.wait_ge(sig["kctx_parts"], at(sig["kctx_parts"], b, 1))
                    spread(kst[2 * st], v.kcp, SC, sig["kctx_filled"], False)
                elif q.kind == "split":
                    sp.wait_ge(sig["split_done"], at(sig["split_done"], b, q.n + 1))
                    if q.x == 0:
                        spread(qst[q.a], v.qp, S, sig["q_filled"], True)
                    else:
                        spread(kst[1], kp, S, sig["k_filled"], False)
                elif q.kind == "rows":
                    nh, h0 = (HG, q.x * HG) if q.a == 1 else (H, 0)
                    sp.wait_ge(sig["act_took"], at(sig["act_took"], b, q.n + 1))
                    sp.dma_start(qst[q.a][MAXROW:P, h0:h0 + nh].rearrange("p h t -> p (h t)"),
                                 v.mT[0:3 * nh, :]).then_inc(sig["rows_filled"], 16)
                    if section == 0 and q.a == 0:
                        constants_of_later_steps()
                elif q.kind == "out":
                    sp.wait_ge(sig1["out_ready"], at(sig1["out_ready"], b, 1))
                    sp.sem_inc(dma_order, 1)
                    sp.dma_start(t["out"][bass.ds(b, 1)].rearrange("o (t p) d -> p (o t) d", p=P), x3[:])\
                        .then_inc(sig1["stored"], 16)

            load(0, 0)
            load(1, 0)
            constants()
            run(sp, body)
            sp.wait_ge(sig0["x_loaded"], 1 + 16 * (B + 1))
            sp.wait_ge(sig0["ctx_loaded"], 1 + 16 * (B + 1))
            sp.wait_ge(sig0["mask_loaded"], 1 + 16 * (B + 1))
            sp.wait_ge(sig1["stored"], 1 + 16 * B)

        @block.gpsimd
        def _(pool):
            start_at_one(pool, "gpsimd")
            for a in range(3):
                nc.gpsimd.memset(vx[a][:], 0.0).then_inc(pool_chain, 1)
            pool.wait_ge(pool_chain, 3)
            for a in range(3):
                nc.gpsimd.memset(vx[a][0:(P if a == 1 else SC), :, :, DK:DK + 1], 1.0).then_inc(padded, 1)
            pool.wait_ge(consts, 16 * N_CONST)

            at = counter(pool)

            def body(b, q, section):
                st, v, sig = q.st, streams[q.st], signals[q.st]
                if q.kind == "stats":
                    pool.wait_ge(sig["var_ready"], at(sig["var_ready"], b, q.n + 1))
                    nc.gpsimd.tensor_tensor(v.rstd[:], v.vareps[:], halfneg[:], ALU.pow)\
                        .then_inc(sig["rstd_ready"], 1)
                elif q.kind == "residual":
                    if q.a == 0:
                        pool.wait_ge(sig0["x_loaded"], at(sig0["x_loaded"], b, 16))
                        pool.wait_ge(sig0["dve_took"], at(sig0["dve_took"], b, 0))
                    elif q.a == 1:
                        pool.wait_ge(sig0["z_ready"], at(sig0["z_ready"], b, 2))
                        pool.wait_ge(sig0["dve_took"], at(sig0["dve_took"], b, find(0, "attn", 0).n + 1))
                    else:
                        pool.wait_ge(sig1["acc_done"], at(sig1["acc_done"], b, NE))
                        pool.wait_ge(sig1["dve_took"], at(sig1["dve_took"], b, 0))
                    x = [x0, u1, x2][q.a]
                    nc.gpsimd.tensor_tensor(v.res[:], x[:], R[f"bo{q.a}"].unsqueeze(1).to_broadcast([P, NT, D]),
                                            ALU.add)\
                        .then_inc(sig["res_ready"], 1)
                    if section == 0 and q.a == 0:
                        pool.wait_ge(sig0["res_ready"], 1 + 1)
                        for k, clear in enumerate((kst[1][P // 2:P], kst[2][:], qst[2][P // 2:P])):
                            if k:
                                pool.wait_ge(cleared1, k)
                            nc.gpsimd.memset(clear.bitcast(I32), 0).then_inc(cleared1, 1)
                        pool.wait_ge(cleared1, 3)

            run(pool, body)

        @block.scalar
        def _(act):
            start_at_one(act, "scalar")
            act.wait_ge(consts, 16 * N_CONST)
            act.wait_ge(cleared, 3)
            act.wait_ge(qbias_ready, 1)

            at = counter(act)

            def body(b, q, _):
                st, v, sig = q.st, streams[q.st], signals[q.st]
                if KINDS[q.kind][0] == "act_took":
                    src = v.ring[q.bank]
                    src_b = src[:, 0:256].bitcast(BF16)
                    act.wait_ge(sig["for_act"], at(sig["for_act"], b, q.n + 1))
                    if q.kind == "ctx":
                        ins = nc.scalar.activation(v.ctxT[:], src[:, 0:SC], ACT.Copy)
                    elif q.kind == "mask":
                        ins = nc.scalar.activation(maskT[0:SC], src_b[0:SC, :], ACT.Copy)
                    elif q.kind == "z" and (st, q.a) in ((0, 1), (1, 0)):
                        g, c = ("g1", "c1") if st == 0 else ("g2", "c2")
                        ins = nc.scalar.activation(v.zT[:], src[:], ACT.Identity, bias=C[c], scale=C[g])
                    elif q.kind in ("z", "o"):
                        ins = nc.scalar.activation(v.zT[:], src[:], ACT.Copy)
                    elif q.kind in ("q", "k"):
                        act.wait_ge(sig["split_done"], at(sig["split_done"], b, find(st, "split", q.a, q.kind == "k").n))
                        if q.kind == "q":
                            ins = nc.scalar.activation(v.lin[:], src[:], ACT.Identity, bias=qbias[:, q.a:q.a + 1],
                                                       scale=QSCALE)
                        else:
                            ins = nc.scalar.activation(v.lin[:], src[:], ACT.Identity, bias=C["bk1"])
                    elif q.kind == "rows":
                        nh = HG if q.a == 1 else H
                        rows = find(st, "parts", q.a, q.x).n
                        act.wait_ge(sig["rows_filled"], at(sig["rows_filled"], b, 16 * rows))
                        ins = nc.scalar.activation(v.mT[0:3 * nh, :], src_b[0:3 * nh, :], ACT.Copy)
                    elif q.kind == "hot":
                        ins = nc.scalar.activation(hotT[:], src[0:NE, :], ACT.Copy)
                    ins.then_inc(sig["act_took"], 1)
                elif q.kind == "exp":
                    rows = P if q.a == 1 else SCP
                    act.wait_ge(sig["scores"], at(sig["scores"], b, q.n + 1))
                    act.wait_ge(sig["pv_done"], at(sig["pv_done"], b, max(q.n - NPROBS[st] + HG, 0) // HG))
                    nc.scalar.activation(v.probs[0:rows, q.n % NPROBS[st]], v.ring[q.bank][0:rows, :], ACT.Exp)\
                        .then_inc(sig["probs"], 1)
                elif q.kind == "strips":
                    groups = G * (q.a if st == 0 else 0) + q.x
                    last = find(st, "pv", q.a, (q.x + 1) * (NT if q.a == 1 else 1) - 1)
                    act.wait_ge(sig["pv_done"], at(sig["pv_done"], b, last.n + 1))
                    before = [s for s in STEPS[st] if s.kind == "heads"]
                    act.wait_ge(sig["for_dve"], at(sig["for_dve"], b, before[groups - 1].n + 1 if groups else 0))
                    nc.scalar.activation(v.strips[:], v.acc[:], ACT.Copy).then_inc(sig["strips_ready"], 1)
                elif q.kind == "up":
                    act.wait_ge(sig["for_mid"], at(sig["for_mid"], b, q.n + 1))
                    act.wait_ge(sig1["down_done"], at(sig1["down_done"], b, max(q.n - NF + 1, 0)))
                    e, f = q.x
                    nc.scalar.activation(mid[:, f], v.ring[q.bank][:], ACT.Relu, bias=b1[:, e, f:f + 1])\
                        .then_inc(sig["mid"], 1)
                elif q.kind == "fup":
                    act.wait_ge(sig["for_mid"], at(sig["for_mid"], b, q.n + 1))
                    nc.scalar.activation(mid[:, q.x], v.ring[q.bank][:], ACT.Gelu_apprx_tanh, bias=fb1[:, q.x:q.x + 1])\
                        .then_inc(sig["mid"], 1)
                elif q.kind == "sigmoid":
                    act.wait_ge(sig1["score_ready"], at(sig1["score_ready"], b, 1))
                    nc.scalar.activation(esig[:], score[:], ACT.Exp, scale=-1.0).then_inc(sig1["sig_ready"], 1)

            run(act, body)

        @block.tensor
        def _(pe):
            start_at_one(pe, "tensor")
            pe.wait_ge(consts, 16 * N_CONST)
            pe.wait_ge(padded, 3)
            pe.wait_ge(cleared, 3)
            waited = [False]

            def transposes(dst, src, eye):
                for k in range(NT):
                    ins = nc.tensor.transpose(dst[:, k * P:(k + 1) * P], src(k), eye)
                return ins

            at = counter(pe)

            def body(b, q, section):
                st, v, sig = q.st, streams[q.st], signals[q.st]
                if st == 1 and not waited[0]:
                    waited[0] = True
                    pe.wait_ge(consts2, 16 * N_CONST2)
                a, x = q.a, q.x
                if q.kind in USES_RING:
                    pe.wait_ge(signals[st][q.freed[0]], at(signals[st][q.freed[0]], b, q.freed[1]))
                    dst = v.ring[q.bank]
                    dst_b = dst[:, 0:256].bitcast(BF16)
                if q.kind == "ctx":
                    pe.wait_ge(sig["ctx_loaded"], at(sig["ctx_loaded"], b, 16))
                    nc.tensor.transpose(dst[:, 0:SC], v.ctx_in[:], ident[0:SC, 0:SC]).then_inc(sig["for_act"], 1)
                elif q.kind == "ctxkv":
                    pe.wait_ge(sig["act_took"], at(sig["act_took"], b, find(st, "ctx").n + 1))
                    nc.tensor.matmul(dst[:, 0:SC], W[f"k{2 * st}"], v.ctxT[:], start=True, stop=True)
                    nc.tensor.matmul(dst[0:SC, D:2 * D], v.ctxT[:], W[f"v{2 * st}"], start=True, stop=True)\
                        .then_inc(sig["for_dve"], 1)
                elif q.kind == "mask":
                    pe.wait_ge(sig0["mask_num"], at(sig0["mask_num"], b, 1))
                    transposes(dst_b[0:SC], lambda k: mask_neg[:, k, :], identb[:]).then_inc(sig["for_act"], 1)
                elif q.kind == "z":
                    norm = [[0, 2], [0, None, 1, 2]][st][a]
                    pe.wait_ge(sig["z_ready"], at(sig["z_ready"], b, norm + 1))
                    transposes(dst, lambda k: v.z[:, k, :], ident[:]).then_inc(sig["for_act"], 1)
                elif q.kind in ("q", "k"):
                    pe.wait_ge(sig["act_took"], at(sig["act_took"], b, find(st, "z", a).n + 1))
                    nc.tensor.matmul(dst[:], W[f"{q.kind}{a}"], v.zT[:], start=True, stop=True)\
                        .then_inc(sig["for_act"], 1)
                elif q.kind == "v":
                    for k in range(NT):
                        ins = nc.tensor.matmul(dst[:, k * P:(k + 1) * P], v.zT[:, k * P:(k + 1) * P], W["v1"],
                                               start=True, stop=True, skip_group_check=True)
                    ins.then_inc(sig["for_dve"], 1)
                elif q.kind == "max":
                    if section == 0 and x == 0:
                        pe.wait_ge([ones, ones1][a], 16)
                    if x == 0:
                        pe.wait_ge(sig["q_filled"], at(sig["q_filled"], b, 16 * 9 * (1 + (a == 1))))
                        filled = sig["k_filled"] if a == 1 else sig["kctx_filled"]
                        pe.wait_ge(filled, at(filled, b, 16 * 9))
                    if a == 1:
                        h, k = divmod(x, NT)
                        ins = nc.tensor.matmul(dst[:], qst[1][0:MAXROW, h, k * P:(k + 1) * P], kst[1][0:MAXROW, h, :],
                                               start=True, stop=True)
                    else:
                        g, k = divmod(x, NT)
                        first = True
                        if a == 0:
                            if x == 0:
                                pe.wait_ge(sig0["act_took"], at(sig0["act_took"], b, find(0, "mask").n + 1))
                            nc.tensor.matmul(dst[:, 0:HG * SC], maskT[0:SC, k * P:(k + 1) * P], eye4[:],
                                             start=True, stop=False, skip_group_check=True)
                            first = False
                        elif k == NT - 1:
                            for part in range(3):
                                nc.tensor.matmul(dst[:, 0:HG * SC], corner[:], slopes[:, part, g * HG:(g + 1) * HG, :],
                                                 start=(part == 0), stop=False, skip_group_check=True)
                            first = False
                        for c in range(HG):
                            h = g * HG + c
                            ins = nc.tensor.matmul(dst[:, c * SC:(c + 1) * SC], qst[a][0:MAXROW, h, k * P:(k + 1) * P],
                                                   kst[a][0:MAXROW, h, 0:SC], start=first and c == 0, stop=True,
                                                   skip_group_check=True)
                    ins.then_inc(sig["max_scores"], 1)
                elif q.kind == "rows":
                    nh = HG if a == 1 else H
                    pe.wait_ge(sig["max_parts"], at(sig["max_parts"], b, find(st, "parts", a, x).n + 1))
                    for k in range(NT):
                        cols = v.negp[:, k].rearrange("p a h -> p (a h)")
                        for r0 in range(0, 3 * nh, 32):
                            r1 = min(3 * nh, r0 + 32)
                            ins = nc.tensor.transpose(dst_b[r0:r1, k * P:(k + 1) * P], cols[:, r0:r1], identb[:])
                    ins.then_inc(sig["for_act"], 1)
                elif q.kind == "exp":
                    if a == 1:
                        g, k, c = x // (HG * NT), x % (HG * NT) // HG, x % HG
                        if x % (HG * NT) == 0:
                            pe.wait_ge(sig["rows_filled"], at(sig["rows_filled"], b, 16 * (find(st, "parts", 1, g).n + 1)))
                    else:
                        g, k, c = x // HG, 0, x % HG
                        if x == 0:
                            pe.wait_ge(sig["rows_filled"], at(sig["rows_filled"], b, 16 * (find(st, "parts", a, 0).n + 1)))
                    m = P if a == 1 else SCP
                    h = g * HG + c
                    if a == 0:
                        nc.tensor.matmul(dst[0:m], identb[0:SCP, 0:SCP], maskT[:], start=True, stop=False,
                                         skip_group_check=True)
                    ins = nc.tensor.matmul(dst[0:m], kst[a][:, h, k * P:k * P + m], qst[a][:, h, :],
                                           start=a != 0, stop=True, skip_group_check=a != 1)
                    if a == 2:
                        for part in range(3):
                            ins = nc.tensor.matmul(dst[0:SC, S - CORNER:S], slopes[:, part, h, :],
                                                   corner[:, P - CORNER:P], start=False, stop=True,
                                                   skip_group_check=True)
                    ins.then_inc(sig["scores"], 1)
                elif q.kind == "pv":
                    pe.wait_ge(sig["probs"], at(sig["probs"], b, HG * (q.n + 1)))
                    g, k = divmod(x, NT) if a == 1 else (x, 0)
                    if k == 0:
                        pe.wait_ge(sig["strips_ready"], at(sig["strips_ready"], b, G * (a if st == 0 else 0) + g))
                        if g == 0:
                            vstep = find(st, "v", 1) if a == 1 else find(st, "ctxkv")
                            pe.wait_ge(sig["dve_took"], at(sig["dve_took"], b, vstep.n + 1))
                            if st == 1:
                                pe.wait_ge(sig1["acc_done"], at(sig1["acc_done"], b, NE))
                    m = P if a == 1 else SCP
                    for c in range(HG):
                        ins = nc.tensor.matmul(v.acc[32 * c:32 * c + 32, :], vx[a][:, k, g * HG + c, :],
                                               v.probs[0:m, (HG * q.n + c) % NPROBS[st], :], start=k == 0,
                                               stop=(k == NT - 1 or a != 1))
                    ins.then_inc(sig["pv_done"], 1)
                elif q.kind == "heads":
                    pe.wait_ge(sig["strips_ready"], at(sig["strips_ready"], b, G * (a if st == 0 else 0) + x + 1))
                    transposes(dst, lambda k: v.strips[:, k * P:(k + 1) * P], ident[:])\
                        .then_inc(sig["for_dve"], 1)
                elif q.kind == "o":
                    pe.wait_ge(sig["dve_took"], at(sig["dve_took"], b, find(st, "heads", a, G - 1).n + 1))
                    transposes(dst, lambda k: v.z[:, k, :], ident[:]).then_inc(sig["for_act"], 1)
                elif q.kind == "attn":
                    pe.wait_ge(sig["act_took"], at(sig["act_took"], b, find(st, "o", a).n + 1))
                    for k in range(NT):
                        ins = nc.tensor.matmul(dst[:, k * P:(k + 1) * P], v.zT[:, k * P:(k + 1) * P], W[f"o{a}"],
                                               start=True, stop=True, skip_group_check=True)
                    ins.then_inc(sig["for_dve"], 1)
                elif q.kind == "logit":
                    pe.wait_ge(sig1["act_took"], at(sig1["act_took"], b, find(1, "z", 0).n + 1))
                    for k in range(NT):
                        ins = nc.tensor.matmul(dst[:, k * NE:(k + 1) * NE], v.zT[:, k * P:(k + 1) * P], gate_w[:],
                                               start=True, stop=True, skip_group_check=True)
                    ins.then_inc(sig1["for_dve"], 1)
                elif q.kind == "hot":
                    pe.wait_ge(sig1["dve_took"], at(sig1["dve_took"], b, find(1, "logit").n + 1))
                    transposes(dst[0:NE], lambda k: hot[:, k, :], ident[:]).then_inc(sig1["for_act"], 1)
                elif q.kind == "bias":
                    pe.wait_ge(sig1["act_took"], at(sig1["act_took"], b, find(1, "hot").n + 1))
                    for k in range(NT):
                        ins = nc.tensor.matmul(dst[:, k * P:(k + 1) * P], hotT[:, k * P:(k + 1) * P], b2[:],
                                               start=True, stop=True, skip_group_check=True)
                    ins.then_inc(sig1["for_dve"], 1)
                elif q.kind in ("up", "fup"):
                    if q.kind == "up":
                        e, f = x
                        weights = w1[:, e, f * P:(f + 1) * P]
                    else:
                        if x == 0:
                            pe.wait_ge(sig1["act_took"], at(sig1["act_took"], b, find(1, "z", 3).n + 1))
                        weights = fw1[:, x * P:(x + 1) * P]
                    nc.tensor.matmul(dst[:], weights, v.zT[:], start=True, stop=True).then_inc(sig1["for_mid"], 1)
                elif q.kind == "down":
                    e, f = x
                    pe.wait_ge(sig1["mid"], at(sig1["mid"], b, q.n + 1))
                    if f == 0:
                        if a == 0 and e == 0:
                            pe.wait_ge(sig1["summed"], at(sig1["summed"], b, 0))
                        elif a == 0:
                            pe.wait_ge(sig1["acc_done"], at(sig1["acc_done"], b, e))
                        else:
                            pe.wait_ge(sig1["strips_ready"], at(sig1["strips_ready"], b, G))
                    weights = w2[:, e, f] if a == 0 else fw2[:, f]
                    for k in range(NT):
                        ins = nc.tensor.matmul(v.acc[:, k * P:(k + 1) * P], mid[:, f, k * P:(k + 1) * P], weights,
                                               start=(f == 0 and k == 0), stop=(f == NF - 1), skip_group_check=True)
                    ins.then_inc(sig1["down_done"], 1)
                elif q.kind == "rank":
                    pe.wait_ge(sig1["score_ready"], at(sig1["score_ready"], b, 1))
                    transposes(dst, lambda k: score[:, k:k + 1].to_broadcast([P, P]), ident[:])\
                        .then_inc(sig1["for_dve"], 1)

            run(pe, body)

        @block.vector
        def _(dve):
            for clear in (kst[0][:], qst01[P // 2:P]):
                nc.vector.memset(clear.bitcast(I32), 0).then_inc(cleared, 1)
            nc.vector.memset(maskT[P // 2:SCP].bitcast(I32), 0).then_inc(cleared, 1)
            start_at_one(dve, "vector")
            dve.wait_ge(consts, 16 * N_CONST)
            dve.wait_ge(cleared, 3)
            nc.vector.tensor_scalar(qbias[:, 0:1], C["bq0"], QSCALE, None, ALU.mult)
            nc.vector.tensor_scalar(qbias[:, 1:2], C["bq1"], QSCALE, None, ALU.mult)
            nc.vector.tensor_scalar(qbias[:, 2:3], C["bq2"], QSCALE, None, ALU.mult).then_inc(qbias_ready, 1)
            dve.wait_ge(padded, 3)
            waited = [False]
            links = [0, 0, 0]
            LINKS = 91

            at = counter(dve)

            def body(b, q, section):
                st, v, sig = q.st, streams[q.st], signals[q.st]
                if st == 1 and not waited[0]:
                    waited[0] = True
                    dve.wait_ge(consts2, 16 * N_CONST2)

                def link(ins):
                    links[section] += 1
                    ins.then_inc(chains[section], 1)
                    turn = (b - 1 if st == 0 else b) if section == 1 else 0
                    dve.wait_ge(chains[section], LINKS * turn + links[section])

                def split(parts, src, rest):
                    link(nc.vector.tensor_copy(parts(0), src))
                    link(nc.vector.tensor_tensor(rest, src, parts(0), ALU.subtract))
                    link(nc.vector.tensor_copy(parts(1), rest))
                    return nc.vector.tensor_tensor(parts(2), rest, parts(1), ALU.subtract)

                a, x = q.a, q.x
                src = v.ring[q.bank] if q.bank is not None else None
                if KINDS[q.kind][0] == "dve_took":
                    dve.wait_ge(sig["for_dve"], at(sig["for_dve"], b, q.n + 1))
                if q.kind == "mask":
                    dve.wait_ge(sig0["mask_loaded"], at(sig0["mask_loaded"], b, 16))
                    dve.wait_ge(sig0["for_act"], at(sig0["for_act"], b, 0))
                    nc.vector.tensor_scalar(mask_neg[:], mask_in[:], 0, -BIG, ALU.is_equal, ALU.mult)\
                        .then_inc(sig0["mask_num"], 1)
                elif q.kind == "ctxkv":
                    dve.wait_ge(sig["kctx_parts"], at(sig["kctx_parts"], b, 0))
                    nc.vector.tensor_scalar(v.kc[:], src[:, 0:SC], C[f"bk{2 * st}"], None, ALU.add)\
                        .then_inc(sig["kctx_lin"], 1)
                    nc.vector.tensor_tensor(
                        vx[2 * st][0:SC, 0, :, 0:DK], src[0:SC, D:2 * D].rearrange("p (h d) -> p h d", d=DK),
                        R[f"bv{2 * st}"][0:SC].rearrange("p (h d) -> p h d", d=DK), ALU.add)\
                        .then_inc(sig["dve_took"], 1)
                elif q.kind == "ctxsplit":
                    dve.wait_ge(sig["kctx_lin"], at(sig["kctx_lin"], b, 1))
                    dve.wait_ge(sig["kctx_filled"], at(sig["kctx_filled"], b, 0))
                    split(lambda p3: v.kcp[:, p3], v.kc[:], v.kcr[:]).then_inc(sig["kctx_parts"], 1)
                elif q.kind == "stats":
                    xin = [[x0, x1, u1], [y, x2, x3]][st][a]
                    if (st, a) == (0, 0):
                        dve.wait_ge(sig0["x_loaded"], at(sig0["x_loaded"], b, 16))
                    elif (st, a) == (0, 1):
                        dve.wait_ge(sig0["dve_took"], at(sig0["dve_took"], b, find(0, "attn", 0).n + 1))
                    elif (st, a) == (1, 0):
                        dve.wait_ge(sig0["dve_took"], at(sig0["dve_took"], b, find(0, "attn", 1).n + 1))
                    elif (st, a) == (1, 1):
                        dve.wait_ge(sig1["acc_done"], at(sig1["acc_done"], b, NE))
                    elif (st, a) == (1, 2):
                        dve.wait_ge(sig1["dve_took"], at(sig1["dve_took"], b, find(1, "attn", 2).n + 1))
                    dve.wait_ge(sig["z_ready"], at(sig["z_ready"], b, q.n))
                    for k in range(NT):
                        ins = nc.vector.bn_stats(v.stats[:, k, :], xin[:, k, :])
                    link(ins)
                    nc.vector.memset(v.vareps[:, 0:1], 0.0)
                    for k in range(NT):
                        ins = nc.vector.bn_aggr(v.meanvar[:, k, :], v.stats[:, k, :])
                    link(ins)
                    nc.vector.tensor_scalar(v.vareps[:], v.meanvar[:, :, 1], EPS, None, ALU.add)\
                        .then_inc(sig["var_ready"], 1)
                elif q.kind == "norm":
                    xin = [[x0, x1, u1], [y, x2, x3]][st][a]
                    dst = u1 if (st, a) == (0, 1) else v.z
                    dve.wait_ge(sig["rstd_ready"], at(sig["rstd_ready"], b, q.n + 1))
                    for k in range(NT):
                        ins = nc.vector.tensor_scalar(dst[:, k, :], xin[:, k, :], v.meanvar[:, k, 0:1],
                                                      v.rstd[:, k:k + 1], ALU.subtract, ALU.mult)
                    ins.then_inc(sig["z_ready"], 1)
                elif q.kind == "split":
                    step = find(st, "q" if x == 0 else "k", a)
                    dve.wait_ge(sig["act_took"], at(sig["act_took"], b, step.n + 1))
                    if x == 0:
                        dve.wait_ge(sig["q_filled"], at(sig["q_filled"], b, 16 * 9 * (a == 1)))
                    else:
                        dve.wait_ge(sig["k_filled"], at(sig["k_filled"], b, 0))
                    parts = v.qp if x == 0 else kp
                    split(lambda p3: parts[:, p3, :], v.lin[:], v.rest[:]).then_inc(sig["split_done"], 1)
                elif q.kind == "v":
                    for k in range(NT):
                        ins = nc.vector.tensor_tensor(vx[1][:, k, :, 0:DK],
                                                      src[:, k * P:(k + 1) * P].rearrange("p (h d) -> p h d", d=DK),
                                                      R["bv1"].rearrange("p (h d) -> p h d", d=DK), ALU.add)
                    ins.then_inc(sig["dve_took"], 1)
                elif q.kind == "max":
                    dve.wait_ge(sig["max_scores"], at(sig["max_scores"], b, q.n + 1))
                    if a == 1:
                        h, k = divmod(x, NT)
                        if x % (HG * NT) == 0:
                            dve.wait_ge(sig["max_parts"], at(sig["max_parts"], b, find(st, "parts", 1, h // HG).n))
                        nc.vector.tensor_reduce(v.negmax[:, k, h % HG:h % HG + 1], src[:], AX.X, ALU.max,
                                                negate=True).then_inc(sig["max_taken"], 1)
                    else:
                        g, k = divmod(x, NT)
                        if x == 0:
                            dve.wait_ge(sig["max_parts"], at(sig["max_parts"], b, 0))
                        nc.vector.tensor_reduce(v.negmax[:, k, g * HG:(g + 1) * HG],
                                                src[:, 0:HG * SC].rearrange("p (h k) -> p h k", k=SC),
                                                AX.X, ALU.max, negate=True).then_inc(sig["max_taken"], 1)
                elif q.kind == "parts":
                    nh = HG if a == 1 else H
                    last = find(st, "max", a, (HG * NT * (x + 1) if a == 1 else G * NT) - 1)
                    dve.wait_ge(sig["max_taken"], at(sig["max_taken"], b, last.n + 1))
                    before = [s for s in STEPS[st] if s.kind == "rows"]
                    dve.wait_ge(sig["for_act"], at(sig["for_act"], b, before[q.n - 1].n + 1 if q.n else 0))
                    parts = v.negp[:].rearrange("p k a h -> p k (a h)")[:, :, 0:3 * nh]\
                        .rearrange("p k (a h) -> p k a h", a=3)
                    split(lambda p3: parts[:, :, p3, :], v.negmax[:, :, 0:nh], v.negrest[:, :, 0:nh])\
                        .then_inc(sig["max_parts"], 1)
                elif q.kind == "heads":
                    dve.wait_ge(sig["dve_took"], at(sig["dve_took"], b, q.n))
                    view = src[:].rearrange("p (t c j) -> p t c j", t=NT, j=32)
                    link(nc.vector.reciprocal(v.rden[:], view[:, :, :, DK]))
                    nc.vector.tensor_tensor(
                        v.z[:].rearrange("p t (g c d) -> p t g c d", g=G, d=DK)[:, :, x],
                        view[:, :, :, 0:DK], v.rden[:].unsqueeze(3).to_broadcast([P, NT, HG, DK]), ALU.mult)\
                        .then_inc(sig["dve_took"], 1)
                elif q.kind == "attn":
                    dve.wait_ge(sig["res_ready"], at(sig["res_ready"], b, find(st, "residual", a).n + 1))
                    dst = [x1, y, x3][a]
                    if st == 0 and section:
                        dve.wait_ge(sig1["base_ready"], at(sig1["base_ready"], b - 1, 1))
                        dve.wait_ge(sig1["z_ready"], at(sig1["z_ready"], b - 1, 1))
                    elif st == 1:
                        dve.wait_ge(sig1["stored"], at(sig1["stored"], b, 0))
                    nc.vector.tensor_tensor(dst[:], src[:].rearrange("p (t d) -> p t d", d=D), v.res[:], ALU.add)\
                        .then_inc(sig["dve_took"], 1)
                elif q.kind == "base":
                    dve.wait_ge(sig1["res_ready"], at(sig1["res_ready"], b, 0))
                    nc.vector.tensor_tensor(x2[:], x1[:], y[:], ALU.add).then_inc(sig1["base_ready"], 1)
                elif q.kind == "logit":
                    link(nc.vector.tensor_tensor(logit[:], src[:, 0:NT * NE].rearrange("p (t e) -> p t e", e=NE),
                                                 gate_b[:].unsqueeze(1).to_broadcast([P, NT, NE]), ALU.add))
                    link(nc.vector.tensor_reduce(top[:], logit[:], AX.X, ALU.max))
                    link(nc.vector.tensor_tensor(pick[:], logit[:], top[:].unsqueeze(2).to_broadcast([P, NT, NE]),
                                                 ALU.is_equal))
                    link(nc.vector.tensor_tensor(pick[:], pick[:],
                                                 falling[:].unsqueeze(1).to_broadcast([P, NT, NE]), ALU.mult))
                    link(nc.vector.tensor_reduce(top[:], pick[:], AX.X, ALU.max))
                    nc.vector.tensor_tensor(hot[:], falling[:].unsqueeze(1).to_broadcast([P, NT, NE]),
                                            top[:].unsqueeze(2).to_broadcast([P, NT, NE]), ALU.is_equal)\
                        .then_inc(sig1["dve_took"], 1)
                elif q.kind == "bias":
                    dve.wait_ge(sig1["base_ready"], at(sig1["base_ready"], b, 1))
                    nc.vector.tensor_tensor(x2[:], x2[:], src[:].rearrange("p (t d) -> p t d", d=D), ALU.add)\
                        .then_inc(sig1["dve_took"], 1)
                elif q.kind == "acc":
                    dve.wait_ge(sig1["down_done"], at(sig1["down_done"], b, NF * (x + 1)))
                    if x:
                        dve.wait_ge(sig1["acc_done"], at(sig1["acc_done"], b, x))
                    else:
                        dve.wait_ge(sig1["dve_took"], at(sig1["dve_took"], b, find(1, "bias").n + 1))
                    for k in range(NT):
                        ins = nc.vector.scalar_tensor_tensor(
                            out=x2[:, k, :], in0=v.acc[:, k * P:(k + 1) * P], scalar=hot[:, k, x:x + 1],
                            in1=x2[:, k, :], op0=ALU.mult, op1=ALU.add)
                    ins.then_inc(sig1["acc_done"], 1)
                elif q.kind == "score":
                    dve.wait_ge(sig1["z_ready"], at(sig1["z_ready"], b, 3))
                    for k in range(NT):
                        link(nc.vector.tensor_tensor(junk[:, 0:D], v.z[:, k, :], R["router"], ALU.mult))
                        ins = nc.vector.tensor_reduce(score[:, k:k + 1], junk[:, 0:D], AX.X, ALU.add)
                        if k + 1 < NT:
                            link(ins)
                    ins.then_inc(sig1["score_ready"], 1)
                elif q.kind == "rank":
                    dve.wait_ge(sig1["score_ready"], at(sig1["score_ready"], b, 1))
                    link(nc.vector.memset(counts[:], 0.0))
                    for k in range(NT):
                        own = score[:, k:k + 1]
                        if k:
                            link(nc.vector.tensor_scalar(junk[:, 0:k * P], src[:, 0:k * P], own, None,
                                                         ALU.is_ge, ALU.add, accum_out=counts[:, k, 0:1]))
                        link(nc.vector.tensor_scalar(junk[:, k * P:S], src[:, k * P:S], own, None,
                                                     ALU.is_gt, ALU.add, accum_out=counts[:, k, 1:2]))
                        link(nc.vector.scalar_tensor_tensor(out=junk[:, 0:P], in0=src[:, k * P:(k + 1) * P],
                                                            scalar=own, in1=lower[:], op0=ALU.is_equal, op1=ALU.mult))
                        link(nc.vector.tensor_reduce(counts[:, k, 2:3], junk[:, 0:P], AX.X, ALU.add))
                    nc.vector.tensor_reduce(rank[:], counts[:], AX.X, ALU.add).then_inc(sig1["dve_took"], 1)
                elif q.kind == "sum":
                    dve.wait_ge(sig1["sig_ready"], at(sig1["sig_ready"], b, 1))
                    dve.wait_ge(sig1["dve_took"], at(sig1["dve_took"], b, find(1, "rank").n + 1))
                    link(nc.vector.tensor_scalar(esig[:], esig[:], 1.0, None, ALU.add))
                    link(nc.vector.reciprocal(weight[:], esig[:]))
                    nc.vector.scalar_tensor_tensor(out=weight[:], in0=rank[:], scalar=float(TOPK) - 0.5,
                                                   in1=weight[:], op0=ALU.is_lt, op1=ALU.mult)\
                        .then_inc(sig1["weight_ready"], 1)
                    link(nc.vector.tensor_tensor(x3[:], x3[:], v.z[:], ALU.add))
                    dve.wait_ge(sig1["down_done"], at(sig1["down_done"], b, NF * NE + NF))
                    nc.vector.tensor_tensor(junk[:].rearrange("p (t d) -> p t d", d=D),
                                            v.acc[:].rearrange("p (t d) -> p t d", d=D),
                                            R["fb2"].unsqueeze(1).to_broadcast([P, NT, D]), ALU.add)\
                        .then_inc(sig1["summed"], 1)
                elif q.kind == "out":
                    dve.wait_ge(sig1["weight_ready"], at(sig1["weight_ready"], b, 1))
                    dve.wait_ge(sig1["summed"], at(sig1["summed"], b, 1))
                    for k in range(NT):
                        ins = nc.vector.scalar_tensor_tensor(
                            out=x3[:, k, :], in0=junk[:, k * P:(k + 1) * P], scalar=weight[:, k:k + 1],
                            in1=x3[:, k, :], op0=ALU.mult, op1=ALU.add)
                    ins.then_inc(sig1["out_ready"], 1)

            run(dve, body)
            assert links[1] == LINKS, links


def shape_constants():
    import numpy as np

    bf = np.dtype("bfloat16")

    def parts(a):
        out, rest = [], a.astype(np.float32)
        for _ in range(3):
            p = rest.astype(bf)
            out.append(p)
            rest = rest - p.astype(np.float32)
        return out

    slope = np.array([2.0 ** (-8.0 * (h + 1) / H) for h in range(H)], np.float32)
    eye = np.eye(SC, dtype=np.float32)
    keys, toks = np.arange(SC, dtype=np.float32), np.arange(S, dtype=np.float32)
    k_lin = parts(-slope[:, None] * (keys + (S - SC))[None, :])
    q_lin = parts(slope[:, None] * toks[None, :])
    one_k, one_q = np.ones((H, SC), bf), np.ones((H, S), bf)
    toks3 = toks[S - P:]
    return {
        "ident": np.eye(P, dtype=np.float32),
        "identb": np.eye(P).astype(bf),
        "eye4": np.ascontiguousarray(np.repeat(eye[:, None, :], HG, 1)).astype(bf),
        "slopes": np.stack([(eye[:, None, :] * p.astype(np.float32)[None, :, None]).astype(bf)
                            for p in parts(-2 * slope)], 1),
        "corner": np.maximum(0, toks3[None, :] - keys[:, None] - (S - SC)).astype(bf),
        "lower": (np.arange(P)[None, :] < np.arange(P)[:, None]).astype(np.float32),
        "falling": np.tile(np.arange(NE, 0, -1).astype(np.float32), (P, 1)),
        "halfneg": np.full((P, NT), -0.5, np.float32),
        "kones": np.ones((3, H, S), bf),
        "kalibi": np.stack(k_lin + [one_k] * 3),
        "qalibi": np.stack([one_q] * 3 + q_lin),
    }


def kernel(**inputs):
    import numpy as np
    import concourse.bacc as bacc
    from concourse.bass_utils import run_bass_kernel_spmd

    a = {k: np.asarray(v) for k, v in inputs.items()}
    dh = np.arange(D).reshape(H, DK).T.reshape(-1)
    x0, f0, x1, f1 = "L0_xattn_", "L0_ffn_", "L1_xattn_", "L1_ffn_"
    wkv, bkv = a[x1 + "Wkv"], a[x1 + "bkv"]
    w = [a[x0 + "W_q"].T[:, dh], a[x0 + "W_k"].T[:, dh], a[x0 + "W_v"].T, a[x0 + "W_o"].T,
         a[f0 + "wq"][:, dh], a[f0 + "wk"][:, dh], a[f0 + "wv"], a[f0 + "wo"],
         a[x1 + "Wq"][:, dh], wkv[:, :D][:, dh], wkv[:, D:], a[x1 + "Wo"]]
    c = [a[x0 + "b_q"][dh], a[x0 + "b_k"][dh], a[f0 + "bq"][dh], a[f0 + "bk"][dh], a[x1 + "bq"][dh], bkv[:D][dh],
         a[f0 + "ln1_g"], a[f0 + "ln1_b"], a[f0 + "ln2_g"], a[f0 + "ln2_b"]]
    r = [a[x0 + "b_v"], a[x0 + "b_o"], a[f0 + "bv"], a[f0 + "bo"], bkv[D:], a[x1 + "bo"], a[f1 + "b2"],
         a[f1 + "w_router"]]
    arrays = {
        "x": a["x"], "ctx": a["ctx_1024"], "mask": a["mask_Bx1xSxS2_ik1"],
        "w": np.stack(w, 1), "c": np.stack(c, 1), "r": np.stack(r, 0),
        "gate_w": a[f0 + "gate_w"], "gate_b": a[f0 + "gate_b"],
        "w1": a[f0 + "w1"].transpose(1, 0, 2),
        "b1": a[f0 + "b1"].reshape(NE, NF, P).transpose(2, 0, 1),
        "w2": a[f0 + "w2"].reshape(NE, NF, P, D).transpose(2, 0, 1, 3),
        "b2": a[f0 + "b2"],
        "fw1": a[f1 + "W1"], "fb1": a[f1 + "b1"].reshape(NF, P).T,
        "fw2": a[f1 + "W2"].reshape(NF, P, D).transpose(1, 0, 2),
    }
    arrays.update(shape_constants())
    arrays = {k: np.ascontiguousarray(v) for k, v in arrays.items()}
    nc = bacc.Bacc("TRN2", target_bir_lowering=False, num_devices=1)
    tensors = {k: nc.dram_tensor(f"in_{k}", v.shape, mybir.dt.from_np(v.dtype), kind="ExternalInput").ap()
               for k, v in arrays.items()}
    tensors["out"] = nc.dram_tensor("out_dram", (B, S, D), F32, kind="ExternalOutput").ap()
    build(nc, tensors)
    result = run_bass_kernel_spmd(nc, [{f"in_{k}": v for k, v in arrays.items()}], core_ids=[0])
    return result.results[0]["out_dram"]
```

```python
from contextlib import ExitStack

import concourse.bass as bass
from concourse import mybir

F32 = mybir.dt.float32
BF16 = mybir.dt.bfloat16
I32 = mybir.dt.int32
ALU = mybir.AluOpType
ACT = mybir.ActivationFunctionType
AX = mybir.AxisListType

B, S, D, SC = 4, 512, 128, 77
H = 16
DK = D // H
P = 128
NT = S // P
G, HG = 4, 4
NE, F = 8, 512
NF = F // P
TOPK = S // 2
EPS = 1e-5
PROD = 9 * DK
ALIBI = 6
CORNER = S - (S - SC) - 1
BIG = 2.0 ** 60
QSCALE = DK ** -0.5
MAXROW = P - 3
SCP = 96

W_NAMES = ["q0", "k0", "v0", "o0", "q1", "k1", "v1", "o1", "q2", "k2", "v2", "o2"]
C_NAMES = ["bq0", "bk0", "bq1", "bk1", "bq2", "bk2", "g1", "c1", "g2", "c2"]
R_NAMES = ["bv0", "bo0", "bv1", "bo1", "bv2", "bo2", "fb2", "router"]

RING = 3
NPROBS = [6, 6]
LEAD = 12

SIGNAL = {
    "ctx": "act_took",
    "mask": "act_took",
    "z": "act_took",
    "q": "act_took",
    "k": "act_took",
    "rows": "act_took",
    "o": "act_took",
    "hot": "act_took",
    "ctxkv": "dve_took",
    "v": "dve_took",
    "heads": "dve_took",
    "attn": "dve_took",
    "logit": "dve_took",
    "bias": "dve_took",
    "rank": "dve_took",
    "max": "max_taken",
    "exp": "probs",
    "up": "mid",
    "fup": "mid",
}
AHEAD = 3


class Step:

    def __init__(self, st, kind, a=0, x=0):
        self.st, self.kind, self.a, self.x = st, kind, a, x
        self.n, self.bank, self.freed = 0, None, None


def attention_steps(st, a):
    steps, groups = [], G
    per = HG * NT if a == 1 else NT
    exps = HG * NT if a == 1 else HG
    emitted = 0

    def add(kind, x=0):
        steps.append(Step(st, kind, a, x))

    def take(n):
        nonlocal emitted
        for _ in range(n):
            if emitted < groups * per:
                add("max", emitted)
            emitted += 1
            if a == 1:
                if emitted % per == 0 and emitted <= groups * per:
                    add("parts", emitted // per - 1)
                if emitted % per == 3 and per < emitted < (groups + 1) * per:
                    add("rows", emitted // per - 1)
    if a == 1:
        take(per + LEAD)
    else:
        take(groups * per)
        add("parts")
        add("rows")
    total = groups * exps
    for e in range(total + 12):
        if e < total:
            add("exp", e)
            if a == 1:
                take(1)
        late = HG + 2 if a == 1 else 0
        if e >= exps + 5 + late and (e - exps - 5 - late) % exps == 0 and (e - exps - 5 - late) // exps < groups:
            add("heads", (e - exps - 5 - late) // exps)
        if e >= 5 and (e - 5) % HG == 0 and (e - 5) // HG < total // HG:
            k = (e - 5) // HG
            add("pv", k)
            if (k + 1) % (exps // HG) == 0:
                add("strips", (k + 1) // (exps // HG) - 1)
    have = {s.x for s in steps if s.kind == "heads"}
    for g in range(groups):
        if g not in have:
            add("heads", g)
    add("o")
    add("attn")
    return steps


def stream_steps(st):
    steps = []

    def add(kind, a=0, x=0):
        steps.append(Step(st, kind, a, x))

    if st == 0:
        add("ctx")
        add("mask")
        add("ctxkv")
        add("stats", 0)
        add("ctxsplit")
        add("norm", 0)
        add("residual", 0)
        add("z", 0)
        add("q", 0)
        add("split", 0, 0)
        add("load")
        steps += attention_steps(0, 0)
        add("stats", 1)
        add("norm", 1)
        add("stats", 2)
        add("residual", 1)
        add("norm", 2)
        add("z", 1)
        add("q", 1)
        add("k", 1)
        add("v", 1)
        add("split", 1, 0)
        add("split", 1, 1)
        steps += attention_steps(0, 1)
    else:
        add("stats", 0)
        add("base")
        add("norm", 0)
        add("z", 0)
        add("ctx")
        add("logit")
        tiles = [(e, f) for e in range(NE) for f in range(NF)]
        for n in range(AHEAD):
            add("up", 0, tiles[n])
        add("hot")
        add("ctxkv")
        add("bias")
        add("ctxsplit")
        add("load")
        for n, (e, f) in enumerate(tiles):
            if n + AHEAD < len(tiles):
                add("up", 0, tiles[n + AHEAD])
            add("down", 0, (e, f))
            if f == NF - 1:
                add("acc", 0, e)
        add("stats", 1)
        add("residual", 2)
        add("norm", 1)
        add("z", 2)
        add("q", 2)
        add("split", 2, 0)
        steps += attention_steps(1, 2)
        add("stats", 2)
        add("norm", 2)
        add("z", 3)
        add("score")
        for f in range(NF):
            add("fup", 0, f)
            if f == 1:
                add("rank")
        add("sigmoid")
        for f in range(NF):
            add("down", 1, (0, f))
        add("sum")
        add("out")
    seen = {}
    for s in steps:
        key = SIGNAL.get(s.kind, s.kind)
        s.n = seen.get(key, 0)
        seen[key] = s.n + 1
    ring = [s for s in steps if s.kind in SIGNAL]
    for u, s in enumerate(ring):
        s.bank = u % RING
        if u >= RING:
            before = ring[u - RING]
            s.freed = (SIGNAL[before.kind], before.n + 1)
        else:
            before = [b for v, b in enumerate(ring) if v % RING == s.bank][-1]
            s.freed = (SIGNAL[before.kind], 0)
    return steps, seen


STEPS, TOTAL = zip(*[stream_steps(st) for st in range(2)])


TURN = [
    0, 1, 2, 2, 2, 2, 1, 3, 2, 1, 1, 2, 2, 9, 1, 5, 17, 2, 1, 4, 14, 1, 3, 1, 9, 1, 2, 1, 1, 1, 2, 5, 1, 2, 1,
    2, 1, 1, 1, 2, 1, 2, 3, 4, 1, 4, 1, 6, 3, 1, 2, 1, 2, 2, 2, 1, 1, 1, 2, 1, 3, 1, 1, 1, 2, 1, 3, 3, 1, 1, 1,
    1, 3, 1, 2, 1, 2, 1, 1, 1, 3, 1, 3, 1, 1, 1, 6, 1, 3, 1, 2, 1, 20, 1, 4, 1, 2, 1, 2, 1, 1, 1, 2, 1, 2, 2, 4,
    6, 2, 2, 2, 1, 5, 1, 8, 1, 2, 1, 1, 1, 1, 1, 1, 1, 1, 2, 2, 2, 2, 1, 1, 2, 1, 1, 1, 1, 1, 1, 2, 1, 3, 1, 1,
    1, 1, 2, 1, 4, 2, 1, 2, 1, 1, 2, 6, 1, 5, 1, 5, 1, 1, 1, 7, 2, 3, 3, 1, 3, 1, 3, 1, 2, 1, 1, 1,
]


def merged():
    assert [sum(TURN[st::2]) for st in range(2)] == [len(steps) for steps in STEPS]
    rest = [iter(steps) for steps in STEPS]
    return [next(rest[k % 2]) for k, run in enumerate(TURN) for _ in range(run)]


def find(st, kind, a=None, x=None):
    return next(s for s in STEPS[st] if s.kind == kind and a in (None, s.a) and x in (None, s.x))


def build(nc, t):
    ctx = ExitStack()

    def sb(name, shape, dt=F32):
        return ctx.enter_context(nc.sbuf_tensor(name, shape, dt))

    def bank(name):
        return ctx.enter_context(nc.psum_tensor(name, [P, 512], F32))

    def sem(name):
        return ctx.enter_context(nc.semaphore(name))

    with ctx:
        w_sb = sb("w_sb", [P, len(W_NAMES), D])
        W = {n: w_sb[:, k, :] for k, n in enumerate(W_NAMES)}
        c_sb = sb("c_sb", [P, len(C_NAMES)])
        C = {n: c_sb[:, k:k + 1] for k, n in enumerate(C_NAMES)}
        qbias = sb("qbias", [P, 3])
        r_sb = sb("r_sb", [P, len(R_NAMES), D])
        R = {n: r_sb[:, k, :] for k, n in enumerate(R_NAMES)}
        gate_w = sb("gate_w", [P, NE])
        gate_b = sb("gate_b", [P, NE])
        w1 = sb("w1", [P, NE, F])
        b1 = sb("b1", [P, NE, NF])
        w2 = sb("w2", [P, NE, NF, D])
        b2 = sb("b2", [NE, D])
        fw1 = sb("fw1", [P, F])
        fb1 = sb("fb1", [P, NF])
        fw2 = sb("fw2", [P, NF, D])
        ident = sb("ident", [P, P])
        identb = sb("identb", [P, P], BF16)
        eye4 = sb("eye4", [SC, HG, SC], BF16)
        lower = sb("lower", [P, P])
        falling = sb("falling", [P, NE])
        halfneg = sb("halfneg", [P, NT])
        slopes = sb("slopes", [SC, 3, H, SC], BF16)
        corner = sb("corner", [SC, P], BF16)

        x0 = sb("x0", [P, NT, D])
        x1 = sb("x1", [P, NT, D])
        u1 = sb("u1", [P, NT, D])
        y = sb("y", [P, NT, D])
        x2 = sb("x2", [P, NT, D])
        x3 = sb("x3", [P, NT, D])
        mask_in = sb("mask_in", [P, NT, SC], I32)
        mask_neg = sb("mask_neg", [P, NT, SC], BF16)
        maskT = sb("maskT", [SCP, S], BF16)
        logit = sb("logit", [P, NT, NE])
        top = sb("top", [P, NT])
        hot = sb("hot", [P, NT, NE])
        pick = sb("pick", [P, NT, NE])
        hotT = sb("hotT", [NE, S])
        score = sb("score", [P, NT])
        junk = sb("junk", [P, S])
        counts = sb("counts", [P, NT, 3])
        rank = sb("rank", [P, NT])
        esig = sb("esig", [P, NT])
        weight = sb("weight", [P, NT])
        kp = sb("kp", [P, 3, S], BF16)
        qst01 = sb("qst01", [P, H, S], BF16)
        qst = [qst01, qst01, sb("qst2", [P, H, S], BF16)]
        kst = [sb("kst0", [P, H, SCP], BF16), sb("kst1", [P, H, S], BF16), sb("kst2", [P, H, SCP], BF16)]
        vx = [sb("vx0", [SCP, 1, H, 32]), sb("vx1", [P, NT, H, 32]), sb("vx2", [SCP, 1, H, 32])]

        class Stream:

            def __init__(self, st):
                def own(name, shape, dt=F32):
                    return sb(f"{name}_{st}", shape, dt)

                self.z = own("z", [P, NT, D])
                self.zT = own("zT", [P, S])
                self.res = own("res", [P, NT, D])
                self.stats = own("stats", [P, NT, 6])
                self.meanvar = own("meanvar", [P, NT, 2])
                self.vareps = own("vareps", [P, NT])
                self.rstd = own("rstd", [P, NT])
                self.lin = own("lin", [P, S])
                self.rest = own("rest", [P, S])
                self.qp = own("qp", [P, 3, S], BF16)
                self.ctx_in = own("ctx_in", [SC, D])
                self.ctxT = own("ctxT", [P, SC])
                self.kc = own("kc", [P, SC])
                self.kcr = own("kcr", [P, SC])
                self.kcp = own("kcp", [P, 3, SC], BF16)
                self.negmax = own("negmax", [P, NT, H])
                self.negrest = own("negrest", [P, NT, H])
                self.negp = own("negp", [P, NT, 3, H], BF16)
                self.mT = own("mT", [3 * H, S], BF16)
                self.probs = own("probs", [P, NPROBS[st], S])
                self.strips = self.lin
                self.rden = own("rden", [P, NT, HG])
                self.ring = [bank(f"ring{st}_{k}") for k in range(RING)]
                self.acc = bank(f"acc{st}")

        streams = [Stream(0), Stream(1)]
        mid = streams[1].probs

        counted = {
            "sync": "x_loaded ctx_loaded mask_loaded kctx_filled q_filled k_filled rows_filled stored",
            "tensor": "for_act for_dve max_scores scores for_mid pv_done down_done",
            "scalar": "act_took probs mid strips_ready sig_ready",
            "vector": "dve_took max_taken mask_num var_ready z_ready split_done kctx_parts kctx_lin max_parts "
                      "base_ready acc_done score_ready weight_ready summed out_ready",
            "gpsimd": "rstd_ready res_ready",
        }
        batch_counts = [{
            "x_loaded": 16 * (1 - st), "ctx_loaded": 16, "mask_loaded": 16 * (1 - st), "kctx_filled": 16 * 9,
            "stored": 16 * st, "q_filled": 16 * 9 * (2 - st), "k_filled": 16 * 9 * (1 - st),
            "rows_filled": 16 * sum(q.kind == "rows" for q in STEPS[st]),
            "for_act": TOTAL[st]["act_took"], "for_dve": TOTAL[st]["dve_took"], "max_scores": TOTAL[st]["max_taken"],
            "scores": TOTAL[st]["probs"], "for_mid": TOTAL[st].get("mid", 0), "pv_done": TOTAL[st]["pv"],
            "down_done": TOTAL[st].get("down", 0), "strips_ready": G * (2 - st), "sig_ready": st,
            "mask_num": 1 - st, "var_ready": 3, "z_ready": 3, "split_done": 3 * TOTAL[st]["split"], "kctx_parts": 3,
            "kctx_lin": 1, "max_parts": 3 * TOTAL[st]["parts"], "base_ready": st, "acc_done": NE * st,
            "score_ready": st, "weight_ready": st, "summed": st, "out_ready": st,
            "rstd_ready": 3, "res_ready": TOTAL[st]["residual"],
            "act_took": TOTAL[st]["act_took"], "dve_took": TOTAL[st]["dve_took"], "max_taken": TOTAL[st]["max_taken"],
            "probs": TOTAL[st]["probs"], "mid": TOTAL[st].get("mid", 0),
        } for st in range(2)]
        signals = [{n: sem(f"{n}_{st}") for names in counted.values() for n in names.split()} for st in range(2)]
        sig0, sig1 = signals
        per_batch = {signals[st][n]: count for st in range(2) for n, count in batch_counts[st].items()}
        consts, consts_later, ones, ones_later, cleared, cleared_later, padded, pool_chain, qbias_ready, dma_order = (
            sem(n) for n in ("consts", "consts_later", "ones", "ones_later", "cleared", "cleared_later", "padded",
                             "pool_chain", "qbias_ready", "dma_order"))
        chains = [sem(f"dve_chain{k}") for k in range(3)]

        def start_at_one(eng, name):
            for st in range(2):
                for n in counted[name].split():
                    eng.sem_inc(signals[st][n], 1)

        def counter(eng):
            def at(semaphore, b, count):
                per = per_batch[semaphore]
                if isinstance(b, int):
                    return per * b + (1 + count)
                value = eng.alloc_register()
                eng.reg_add(value, eng.to_reg(per * b), 1 + count)
                return value
            return at

        def run(eng, body):
            for q in STEPS[0]:
                body(0, q, 0)
            with eng.Fori(0, B - 1) as j:
                for q in merged():
                    body(j + 1 if q.st == 0 else j, q, 1)
            for q in STEPS[1]:
                body(B - 1, q, 2)

        N_CONST, N_CONST_LATER = 7, 16
        block = ctx.enter_context(nc.Block())

        @block.sync
        def _(sp):
            start_at_one(sp, "sync")

            def load(st, b):
                if st == 0:
                    sp.dma_start(x0[:], t["x"][bass.ds(b, 1)].rearrange("o (t p) d -> p (o t) d", p=P))\
                        .then_inc(sig0["x_loaded"], 16)
                sp.dma_start(streams[st].ctx_in[:], t["ctx"][bass.ds(b, 1)].rearrange("o k d -> (o k) d"))\
                    .then_inc(signals[st]["ctx_loaded"], 16)
                if st == 0:
                    sp.dma_start(mask_in[:], t["mask"][bass.ds(b, 1)].rearrange("o e (t p) k -> p (o e t) k", p=P))\
                        .then_inc(sig0["mask_loaded"], 16)

            def constants():
                for dst, name in [(ident, "ident"), (halfneg, "halfneg"), (c_sb, "c"), (w_sb, "w"),
                                  (identb, "identb"), (eye4, "eye4")]:
                    sp.dma_start(dst[:], t[name]).then_inc(consts, 16)
                sp.dma_start(r_sb[:], t["r"].partition_broadcast(P)).then_inc(consts, 16)
                sp.wait_ge(cleared, 3)
                sp.dma_start(kst[0][MAXROW:P, :, 0:SC], t["kones"][:, :, 0:SC]).then_inc(ones, 16)

            def constants_of_later_steps():
                sp.wait_ge(cleared_later, 3)
                sp.dma_start(kst[1][MAXROW:P], t["kones"]).then_inc(ones_later, 16)
                sp.dma_start(kst[2][PROD:PROD + ALIBI, :, 0:SC], t["kalibi"]).then_inc(consts_later, 16)
                sp.dma_start(kst[2][MAXROW:P, :, 0:SC], t["kones"][:, :, 0:SC]).then_inc(consts_later, 16)
                sp.dma_start(qst[2][PROD:PROD + ALIBI], t["qalibi"]).then_inc(consts_later, 16)
                sp.dma_start(gate_b[:], t["gate_b"].partition_broadcast(P)).then_inc(consts_later, 16)
                for dst, name in [(slopes, "slopes"), (corner, "corner"), (fb1, "fb1"), (b1, "b1"), (b2, "b2"),
                                  (gate_w, "gate_w"), (lower, "lower"), (falling, "falling"), (w1, "w1"), (w2, "w2"),
                                  (fw1, "fw1"), (fw2, "fw2")]:
                    sp.dma_start(dst[:], t[name]).then_inc(consts_later, 16)

            def spread(dst, parts, width, filled, is_query, ready, b, before):
                for part in range(3):
                    sp.wait_ge(ready, at(ready, b, before + part + 1))
                    for other in range(3):
                        row = (part * 3 + other if is_query else other * 3 + part) * DK
                        to = dst[row:row + DK, :, 0:width]
                        sp.dma_start(to.rearrange("d h t -> d (h t)") if width == S else to,
                                     parts[:, part, :]).then_inc(filled, 16)

            at = counter(sp)

            def body(b, q, section):
                st, v, sig = q.st, streams[q.st], signals[q.st]
                if q.kind == "load":
                    if section < 2:
                        took = at(sig["for_act"], b, find(st, "ctx").n + 1)
                        if st == 0:
                            masked, added = at(sig0["mask_num"], b, 1), at(sig0["res_ready"], b, 1)
                            normed = at(sig0["z_ready"], b, 1)
                            sp.wait_ge(sig0["mask_num"], masked)
                            sp.wait_ge(sig0["res_ready"], added)
                            sp.wait_ge(sig0["z_ready"], normed)
                        sp.wait_ge(sig["for_act"], took)
                        sp.sem_inc(dma_order, 1)
                        load(st, (b + 1) % B if st == 0 else b + 1)
                elif q.kind == "ctxsplit":
                    spread(kst[2 * st], v.kcp, SC, sig["kctx_filled"], False, sig["kctx_parts"], b, 0)
                elif q.kind == "split":
                    if q.x == 0:
                        spread(qst[q.a], v.qp, S, sig["q_filled"], True, sig["split_done"], b, 3 * q.n)
                    else:
                        spread(kst[1], kp, S, sig["k_filled"], False, sig["split_done"], b, 3 * q.n)
                elif q.kind == "rows":
                    nh, h0 = (HG, q.x * HG) if q.a == 1 else (H, 0)
                    sp.wait_ge(sig["act_took"], at(sig["act_took"], b, q.n + 1))
                    sp.dma_start(qst[q.a][MAXROW:P, h0:h0 + nh].rearrange("p h t -> p (h t)"),
                                 v.mT[0:3 * nh, :]).then_inc(sig["rows_filled"], 16)
                    if section == 0 and q.a == 0:
                        constants_of_later_steps()
                elif q.kind == "out":
                    sp.wait_ge(sig1["out_ready"], at(sig1["out_ready"], b, 1))
                    sp.sem_inc(dma_order, 1)
                    sp.dma_start(t["out"][bass.ds(b, 1)].rearrange("o (t p) d -> p (o t) d", p=P), x3[:])\
                        .then_inc(sig1["stored"], 16)

            load(0, 0)
            load(1, 0)
            constants()
            run(sp, body)
            sp.wait_ge(sig0["x_loaded"], 1 + 16 * (B + 1))
            sp.wait_ge(sig0["ctx_loaded"], 1 + 16 * (B + 1))
            sp.wait_ge(sig0["mask_loaded"], 1 + 16 * (B + 1))
            sp.wait_ge(sig1["stored"], 1 + 16 * B)

        @block.gpsimd
        def _(pool):
            start_at_one(pool, "gpsimd")
            for a in range(3):
                nc.gpsimd.memset(vx[a][:], 0.0).then_inc(pool_chain, 1)
            pool.wait_ge(pool_chain, 3)
            for a in range(3):
                nc.gpsimd.memset(vx[a][0:(P if a == 1 else SC), :, :, DK:DK + 1], 1.0).then_inc(padded, 1)
            pool.wait_ge(consts, 16 * N_CONST)

            at = counter(pool)

            def body(b, q, section):
                st, v, sig = q.st, streams[q.st], signals[q.st]
                if q.kind == "stats":
                    pool.wait_ge(sig["var_ready"], at(sig["var_ready"], b, q.n + 1))
                    nc.gpsimd.tensor_tensor(v.rstd[:], v.vareps[:], halfneg[:], ALU.pow)\
                        .then_inc(sig["rstd_ready"], 1)
                elif q.kind == "residual":
                    if q.a == 0:
                        pool.wait_ge(sig0["x_loaded"], at(sig0["x_loaded"], b, 16))
                        pool.wait_ge(sig0["dve_took"], at(sig0["dve_took"], b, 0))
                    elif q.a == 1:
                        pool.wait_ge(sig0["z_ready"], at(sig0["z_ready"], b, 2))
                        pool.wait_ge(sig0["dve_took"], at(sig0["dve_took"], b, find(0, "attn", 0).n + 1))
                    else:
                        pool.wait_ge(sig1["acc_done"], at(sig1["acc_done"], b, NE))
                        pool.wait_ge(sig1["dve_took"], at(sig1["dve_took"], b, 0))
                    x = [x0, u1, x2][q.a]
                    nc.gpsimd.tensor_tensor(v.res[:], x[:], R[f"bo{q.a}"].unsqueeze(1).to_broadcast([P, NT, D]),
                                            ALU.add)\
                        .then_inc(sig["res_ready"], 1)
                    if section == 0 and q.a == 0:
                        pool.wait_ge(sig0["res_ready"], 1 + 1)
                        for k, clear in enumerate((kst[1][P // 2:P], kst[2][:], qst[2][P // 2:P])):
                            if k:
                                pool.wait_ge(cleared_later, k)
                            nc.gpsimd.memset(clear.bitcast(I32), 0).then_inc(cleared_later, 1)
                        pool.wait_ge(cleared_later, 3)

            run(pool, body)

        @block.scalar
        def _(act):
            start_at_one(act, "scalar")
            act.wait_ge(consts, 16 * N_CONST)
            act.wait_ge(cleared, 3)
            act.wait_ge(qbias_ready, 1)

            at = counter(act)

            def body(b, q, _):
                st, v, sig = q.st, streams[q.st], signals[q.st]
                if SIGNAL.get(q.kind) == "act_took":
                    src = v.ring[q.bank]
                    src_b = src[:, 0:256].bitcast(BF16)
                    act.wait_ge(sig["for_act"], at(sig["for_act"], b, q.n + 1))
                    if q.kind == "ctx":
                        ins = nc.scalar.activation(v.ctxT[:], src[:, 0:SC], ACT.Copy)
                    elif q.kind == "mask":
                        ins = nc.scalar.activation(maskT[0:SC], src_b[0:SC, :], ACT.Copy)
                    elif q.kind == "z" and (st, q.a) in ((0, 1), (1, 0)):
                        g, c = ("g1", "c1") if st == 0 else ("g2", "c2")
                        ins = nc.scalar.activation(v.zT[:], src[:], ACT.Identity, bias=C[c], scale=C[g])
                    elif q.kind in ("z", "o"):
                        ins = nc.scalar.activation(v.zT[:], src[:], ACT.Copy)
                    elif q.kind in ("q", "k"):
                        split = find(st, "split", q.a, q.kind == "k")
                        act.wait_ge(sig["split_done"], at(sig["split_done"], b, 3 * split.n))
                        if q.kind == "q":
                            ins = nc.scalar.activation(v.lin[:], src[:], ACT.Identity, bias=qbias[:, q.a:q.a + 1],
                                                       scale=QSCALE)
                        else:
                            ins = nc.scalar.activation(v.lin[:], src[:], ACT.Identity, bias=C["bk1"])
                    elif q.kind == "rows":
                        nh = HG if q.a == 1 else H
                        rows = find(st, "parts", q.a, q.x).n
                        act.wait_ge(sig["rows_filled"], at(sig["rows_filled"], b, 16 * rows))
                        ins = nc.scalar.activation(v.mT[0:3 * nh, :], src_b[0:3 * nh, :], ACT.Copy)
                    elif q.kind == "hot":
                        ins = nc.scalar.activation(hotT[:], src[0:NE, :], ACT.Copy)
                    ins.then_inc(sig["act_took"], 1)
                elif q.kind == "exp":
                    rows = P if q.a == 1 else SCP
                    act.wait_ge(sig["scores"], at(sig["scores"], b, q.n + 1))
                    act.wait_ge(sig["pv_done"], at(sig["pv_done"], b, max(q.n - NPROBS[st] + HG, 0) // HG))
                    nc.scalar.activation(v.probs[0:rows, q.n % NPROBS[st]], v.ring[q.bank][0:rows, :], ACT.Exp)\
                        .then_inc(sig["probs"], 1)
                elif q.kind == "strips":
                    groups = G * (q.a if st == 0 else 0) + q.x
                    last = find(st, "pv", q.a, (q.x + 1) * (NT if q.a == 1 else 1) - 1)
                    act.wait_ge(sig["pv_done"], at(sig["pv_done"], b, last.n + 1))
                    before = [s for s in STEPS[st] if s.kind == "heads"]
                    act.wait_ge(sig["for_dve"], at(sig["for_dve"], b, before[groups - 1].n + 1 if groups else 0))
                    nc.scalar.activation(v.strips[:], v.acc[:], ACT.Copy).then_inc(sig["strips_ready"], 1)
                elif q.kind == "up":
                    act.wait_ge(sig["for_mid"], at(sig["for_mid"], b, q.n + 1))
                    act.wait_ge(sig1["down_done"], at(sig1["down_done"], b, max(q.n - NF + 1, 0)))
                    e, f = q.x
                    nc.scalar.activation(mid[:, f], v.ring[q.bank][:], ACT.Relu, bias=b1[:, e, f:f + 1])\
                        .then_inc(sig["mid"], 1)
                elif q.kind == "fup":
                    act.wait_ge(sig["for_mid"], at(sig["for_mid"], b, q.n + 1))
                    nc.scalar.activation(mid[:, q.x], v.ring[q.bank][:], ACT.Gelu_apprx_tanh, bias=fb1[:, q.x:q.x + 1])\
                        .then_inc(sig["mid"], 1)
                elif q.kind == "sigmoid":
                    act.wait_ge(sig1["score_ready"], at(sig1["score_ready"], b, 1))
                    nc.scalar.activation(esig[:], score[:], ACT.Exp, scale=-1.0).then_inc(sig1["sig_ready"], 1)

            run(act, body)

        @block.tensor
        def _(pe):
            start_at_one(pe, "tensor")
            pe.wait_ge(consts, 16 * N_CONST)
            pe.wait_ge(padded, 3)
            pe.wait_ge(cleared, 3)
            waited = [False]

            def transposes(dst, src, eye):
                for k in range(NT):
                    ins = nc.tensor.transpose(dst[:, k * P:(k + 1) * P], src(k), eye)
                return ins

            at = counter(pe)

            def body(b, q, section):
                st, v, sig = q.st, streams[q.st], signals[q.st]
                if st == 1 and not waited[0]:
                    waited[0] = True
                    pe.wait_ge(consts_later, 16 * N_CONST_LATER)
                a, x = q.a, q.x
                if q.kind in SIGNAL:
                    pe.wait_ge(signals[st][q.freed[0]], at(signals[st][q.freed[0]], b, q.freed[1]))
                    dst = v.ring[q.bank]
                    dst_b = dst[:, 0:256].bitcast(BF16)
                if q.kind == "ctx":
                    pe.wait_ge(sig["ctx_loaded"], at(sig["ctx_loaded"], b, 16))
                    nc.tensor.transpose(dst[:, 0:SC], v.ctx_in[:], ident[0:SC, 0:SC]).then_inc(sig["for_act"], 1)
                elif q.kind == "ctxkv":
                    pe.wait_ge(sig["act_took"], at(sig["act_took"], b, find(st, "ctx").n + 1))
                    nc.tensor.matmul(dst[:, 0:SC], W[f"k{2 * st}"], v.ctxT[:], start=True, stop=True)
                    nc.tensor.matmul(dst[0:SC, D:2 * D], v.ctxT[:], W[f"v{2 * st}"], start=True, stop=True)\
                        .then_inc(sig["for_dve"], 1)
                elif q.kind == "mask":
                    pe.wait_ge(sig0["mask_num"], at(sig0["mask_num"], b, 1))
                    transposes(dst_b[0:SC], lambda k: mask_neg[:, k, :], identb[:]).then_inc(sig["for_act"], 1)
                elif q.kind == "z":
                    norm = [[0, 2], [0, None, 1, 2]][st][a]
                    pe.wait_ge(sig["z_ready"], at(sig["z_ready"], b, norm + 1))
                    transposes(dst, lambda k: v.z[:, k, :], ident[:]).then_inc(sig["for_act"], 1)
                elif q.kind in ("q", "k"):
                    pe.wait_ge(sig["act_took"], at(sig["act_took"], b, find(st, "z", a).n + 1))
                    nc.tensor.matmul(dst[:], W[f"{q.kind}{a}"], v.zT[:], start=True, stop=True)\
                        .then_inc(sig["for_act"], 1)
                elif q.kind == "v":
                    for k in range(NT):
                        ins = nc.tensor.matmul(dst[:, k * P:(k + 1) * P], v.zT[:, k * P:(k + 1) * P], W["v1"],
                                               start=True, stop=True, skip_group_check=True)
                    ins.then_inc(sig["for_dve"], 1)
                elif q.kind == "max":
                    if section == 0 and x == 0:
                        pe.wait_ge([ones, ones_later][a], 16)
                    if x == 0:
                        pe.wait_ge(sig["q_filled"], at(sig["q_filled"], b, 16 * 9 * (1 + (a == 1))))
                        filled = sig["k_filled"] if a == 1 else sig["kctx_filled"]
                        pe.wait_ge(filled, at(filled, b, 16 * 9))
                    if a == 1:
                        h, k = divmod(x, NT)
                        ins = nc.tensor.matmul(dst[:], qst[1][0:MAXROW, h, k * P:(k + 1) * P], kst[1][0:MAXROW, h, :],
                                               start=True, stop=True)
                    else:
                        g, k = divmod(x, NT)
                        first = True
                        if a == 0:
                            if x == 0:
                                pe.wait_ge(sig0["act_took"], at(sig0["act_took"], b, find(0, "mask").n + 1))
                            nc.tensor.matmul(dst[:, 0:HG * SC], maskT[0:SC, k * P:(k + 1) * P], eye4[:],
                                             start=True, stop=False, skip_group_check=True)
                            first = False
                        elif k == NT - 1:
                            for part in range(3):
                                nc.tensor.matmul(dst[:, 0:HG * SC], corner[:], slopes[:, part, g * HG:(g + 1) * HG, :],
                                                 start=(part == 0), stop=False, skip_group_check=True)
                            first = False
                        for c in range(HG):
                            h = g * HG + c
                            ins = nc.tensor.matmul(dst[:, c * SC:(c + 1) * SC], qst[a][0:MAXROW, h, k * P:(k + 1) * P],
                                                   kst[a][0:MAXROW, h, 0:SC], start=first and c == 0, stop=True,
                                                   skip_group_check=True)
                    ins.then_inc(sig["max_scores"], 1)
                elif q.kind == "rows":
                    nh = HG if a == 1 else H
                    pe.wait_ge(sig["max_parts"], at(sig["max_parts"], b, 3 * (find(st, "parts", a, x).n + 1)))
                    for k in range(NT):
                        cols = v.negp[:, k].rearrange("p a h -> p (a h)")
                        for r0 in range(0, 3 * nh, 32):
                            r1 = min(3 * nh, r0 + 32)
                            ins = nc.tensor.transpose(dst_b[r0:r1, k * P:(k + 1) * P], cols[:, r0:r1], identb[:])
                    ins.then_inc(sig["for_act"], 1)
                elif q.kind == "exp":
                    if a == 1:
                        g, k, c = x // (HG * NT), x % (HG * NT) // HG, x % HG
                        if x % (HG * NT) == 0:
                            rows = find(st, "parts", 1, g).n + 1
                            pe.wait_ge(sig["rows_filled"], at(sig["rows_filled"], b, 16 * rows))
                    else:
                        g, k, c = x // HG, 0, x % HG
                        if x == 0:
                            rows = find(st, "parts", a, 0).n + 1
                            pe.wait_ge(sig["rows_filled"], at(sig["rows_filled"], b, 16 * rows))
                    m = P if a == 1 else SCP
                    h = g * HG + c
                    if a == 0:
                        nc.tensor.matmul(dst[0:m], identb[0:SCP, 0:SCP], maskT[:], start=True, stop=False,
                                         skip_group_check=True)
                    ins = nc.tensor.matmul(dst[0:m], kst[a][:, h, k * P:k * P + m], qst[a][:, h, :],
                                           start=a != 0, stop=True, skip_group_check=a != 1)
                    if a == 2:
                        for part in range(3):
                            ins = nc.tensor.matmul(dst[0:SC, S - CORNER:S], slopes[:, part, h, :],
                                                   corner[:, P - CORNER:P], start=False, stop=True,
                                                   skip_group_check=True)
                    ins.then_inc(sig["scores"], 1)
                elif q.kind == "pv":
                    pe.wait_ge(sig["probs"], at(sig["probs"], b, HG * (q.n + 1)))
                    g, k = divmod(x, NT) if a == 1 else (x, 0)
                    if k == 0:
                        pe.wait_ge(sig["strips_ready"], at(sig["strips_ready"], b, G * (a if st == 0 else 0) + g))
                        if g == 0:
                            vstep = find(st, "v", 1) if a == 1 else find(st, "ctxkv")
                            pe.wait_ge(sig["dve_took"], at(sig["dve_took"], b, vstep.n + 1))
                            if st == 1:
                                pe.wait_ge(sig1["acc_done"], at(sig1["acc_done"], b, NE))
                    m = P if a == 1 else SCP
                    for c in range(HG):
                        ins = nc.tensor.matmul(v.acc[32 * c:32 * c + 32, :], vx[a][:, k, g * HG + c, :],
                                               v.probs[0:m, (HG * q.n + c) % NPROBS[st], :], start=k == 0,
                                               stop=(k == NT - 1 or a != 1))
                    ins.then_inc(sig["pv_done"], 1)
                elif q.kind == "heads":
                    pe.wait_ge(sig["strips_ready"], at(sig["strips_ready"], b, G * (a if st == 0 else 0) + x + 1))
                    transposes(dst, lambda k: v.strips[:, k * P:(k + 1) * P], ident[:])\
                        .then_inc(sig["for_dve"], 1)
                elif q.kind == "o":
                    pe.wait_ge(sig["dve_took"], at(sig["dve_took"], b, find(st, "heads", a, G - 1).n + 1))
                    transposes(dst, lambda k: v.z[:, k, :], ident[:]).then_inc(sig["for_act"], 1)
                elif q.kind == "attn":
                    pe.wait_ge(sig["act_took"], at(sig["act_took"], b, find(st, "o", a).n + 1))
                    for k in range(NT):
                        ins = nc.tensor.matmul(dst[:, k * P:(k + 1) * P], v.zT[:, k * P:(k + 1) * P], W[f"o{a}"],
                                               start=True, stop=True, skip_group_check=True)
                    ins.then_inc(sig["for_dve"], 1)
                elif q.kind == "logit":
                    pe.wait_ge(sig1["act_took"], at(sig1["act_took"], b, find(1, "z", 0).n + 1))
                    for k in range(NT):
                        ins = nc.tensor.matmul(dst[:, k * NE:(k + 1) * NE], v.zT[:, k * P:(k + 1) * P], gate_w[:],
                                               start=True, stop=True, skip_group_check=True)
                    ins.then_inc(sig1["for_dve"], 1)
                elif q.kind == "hot":
                    pe.wait_ge(sig1["dve_took"], at(sig1["dve_took"], b, find(1, "logit").n + 1))
                    transposes(dst[0:NE], lambda k: hot[:, k, :], ident[:]).then_inc(sig1["for_act"], 1)
                elif q.kind == "bias":
                    pe.wait_ge(sig1["act_took"], at(sig1["act_took"], b, find(1, "hot").n + 1))
                    for k in range(NT):
                        ins = nc.tensor.matmul(dst[:, k * P:(k + 1) * P], hotT[:, k * P:(k + 1) * P], b2[:],
                                               start=True, stop=True, skip_group_check=True)
                    ins.then_inc(sig1["for_dve"], 1)
                elif q.kind in ("up", "fup"):
                    if q.kind == "up":
                        e, f = x
                        weights = w1[:, e, f * P:(f + 1) * P]
                    else:
                        if x == 0:
                            pe.wait_ge(sig1["act_took"], at(sig1["act_took"], b, find(1, "z", 3).n + 1))
                        weights = fw1[:, x * P:(x + 1) * P]
                    nc.tensor.matmul(dst[:], weights, v.zT[:], start=True, stop=True).then_inc(sig1["for_mid"], 1)
                elif q.kind == "down":
                    e, f = x
                    pe.wait_ge(sig1["mid"], at(sig1["mid"], b, q.n + 1))
                    if f == 0:
                        if a == 0 and e == 0:
                            pe.wait_ge(sig1["summed"], at(sig1["summed"], b, 0))
                        elif a == 0:
                            pe.wait_ge(sig1["acc_done"], at(sig1["acc_done"], b, e))
                        else:
                            pe.wait_ge(sig1["strips_ready"], at(sig1["strips_ready"], b, G))
                    weights = w2[:, e, f] if a == 0 else fw2[:, f]
                    for k in range(NT):
                        ins = nc.tensor.matmul(v.acc[:, k * P:(k + 1) * P], mid[:, f, k * P:(k + 1) * P], weights,
                                               start=(f == 0 and k == 0), stop=(f == NF - 1), skip_group_check=True)
                    ins.then_inc(sig1["down_done"], 1)
                elif q.kind == "rank":
                    pe.wait_ge(sig1["score_ready"], at(sig1["score_ready"], b, 1))
                    transposes(dst, lambda k: score[:, k:k + 1].to_broadcast([P, P]), ident[:])\
                        .then_inc(sig1["for_dve"], 1)

            run(pe, body)

        @block.vector
        def _(dve):
            for clear in (kst[0][:], qst01[P // 2:P]):
                nc.vector.memset(clear.bitcast(I32), 0).then_inc(cleared, 1)
            nc.vector.memset(maskT[P // 2:SCP].bitcast(I32), 0).then_inc(cleared, 1)
            start_at_one(dve, "vector")
            dve.wait_ge(consts, 16 * N_CONST)
            dve.wait_ge(cleared, 3)
            nc.vector.tensor_scalar(qbias[:, 0:1], C["bq0"], QSCALE, None, ALU.mult)
            nc.vector.tensor_scalar(qbias[:, 1:2], C["bq1"], QSCALE, None, ALU.mult)
            nc.vector.tensor_scalar(qbias[:, 2:3], C["bq2"], QSCALE, None, ALU.mult).then_inc(qbias_ready, 1)
            dve.wait_ge(padded, 3)
            waited = [False]
            links = [0, 0, 0]
            LINKS = 67

            at = counter(dve)

            def body(b, q, section):
                st, v, sig = q.st, streams[q.st], signals[q.st]
                if st == 1 and not waited[0]:
                    waited[0] = True
                    dve.wait_ge(consts_later, 16 * N_CONST_LATER)

                def link(ins):
                    links[section] += 1
                    ins.then_inc(chains[section], 1)
                    turn = (b - 1 if st == 0 else b) if section == 1 else 0
                    dve.wait_ge(chains[section], LINKS * turn + links[section])

                def split(parts, src, rest, ready, before):
                    nc.vector.tensor_copy(parts(0), src).then_inc(ready, 1)
                    dve.wait_ge(ready, at(ready, b, before + 1))
                    link(nc.vector.tensor_tensor(rest, src, parts(0), ALU.subtract))
                    nc.vector.tensor_copy(parts(1), rest).then_inc(ready, 1)
                    dve.wait_ge(ready, at(ready, b, before + 2))
                    nc.vector.tensor_tensor(parts(2), rest, parts(1), ALU.subtract).then_inc(ready, 1)

                a, x = q.a, q.x
                src = v.ring[q.bank] if q.bank is not None else None
                if SIGNAL.get(q.kind) == "dve_took":
                    dve.wait_ge(sig["for_dve"], at(sig["for_dve"], b, q.n + 1))
                if q.kind == "mask":
                    dve.wait_ge(sig0["mask_loaded"], at(sig0["mask_loaded"], b, 16))
                    dve.wait_ge(sig0["for_act"], at(sig0["for_act"], b, 0))
                    nc.vector.tensor_scalar(mask_neg[:], mask_in[:], 0, -BIG, ALU.is_equal, ALU.mult)\
                        .then_inc(sig0["mask_num"], 1)
                elif q.kind == "ctxkv":
                    dve.wait_ge(sig["kctx_parts"], at(sig["kctx_parts"], b, 0))
                    nc.vector.tensor_scalar(v.kc[:], src[:, 0:SC], C[f"bk{2 * st}"], None, ALU.add)\
                        .then_inc(sig["kctx_lin"], 1)
                    nc.vector.tensor_tensor(
                        vx[2 * st][0:SC, 0, :, 0:DK], src[0:SC, D:2 * D].rearrange("p (h d) -> p h d", d=DK),
                        R[f"bv{2 * st}"][0:SC].rearrange("p (h d) -> p h d", d=DK), ALU.add)\
                        .then_inc(sig["dve_took"], 1)
                elif q.kind == "ctxsplit":
                    dve.wait_ge(sig["kctx_lin"], at(sig["kctx_lin"], b, 1))
                    dve.wait_ge(sig["kctx_filled"], at(sig["kctx_filled"], b, 0))
                    split(lambda p3: v.kcp[:, p3], v.kc[:], v.kcr[:], sig["kctx_parts"], 0)
                elif q.kind == "stats":
                    xin = [[x0, x1, u1], [y, x2, x3]][st][a]
                    if (st, a) == (0, 0):
                        dve.wait_ge(sig0["x_loaded"], at(sig0["x_loaded"], b, 16))
                    elif (st, a) == (0, 1):
                        dve.wait_ge(sig0["dve_took"], at(sig0["dve_took"], b, find(0, "attn", 0).n + 1))
                    elif (st, a) == (1, 0):
                        dve.wait_ge(sig0["dve_took"], at(sig0["dve_took"], b, find(0, "attn", 1).n + 1))
                    elif (st, a) == (1, 1):
                        dve.wait_ge(sig1["acc_done"], at(sig1["acc_done"], b, NE))
                    elif (st, a) == (1, 2):
                        dve.wait_ge(sig1["dve_took"], at(sig1["dve_took"], b, find(1, "attn", 2).n + 1))
                    dve.wait_ge(sig["z_ready"], at(sig["z_ready"], b, q.n))
                    for k in range(NT):
                        ins = nc.vector.bn_stats(v.stats[:, k, :], xin[:, k, :])
                    link(ins)
                    nc.vector.memset(v.vareps[:, 0:1], 0.0)
                    for k in range(NT):
                        ins = nc.vector.bn_aggr(v.meanvar[:, k, :], v.stats[:, k, :])
                    link(ins)
                    nc.vector.tensor_scalar(v.vareps[:], v.meanvar[:, :, 1], EPS, None, ALU.add)\
                        .then_inc(sig["var_ready"], 1)
                elif q.kind == "norm":
                    xin = [[x0, x1, u1], [y, x2, x3]][st][a]
                    dst = u1 if (st, a) == (0, 1) else v.z
                    dve.wait_ge(sig["rstd_ready"], at(sig["rstd_ready"], b, q.n + 1))
                    for k in range(NT):
                        ins = nc.vector.tensor_scalar(dst[:, k, :], xin[:, k, :], v.meanvar[:, k, 0:1],
                                                      v.rstd[:, k:k + 1], ALU.subtract, ALU.mult)
                    ins.then_inc(sig["z_ready"], 1)
                elif q.kind == "split":
                    step = find(st, "q" if x == 0 else "k", a)
                    dve.wait_ge(sig["act_took"], at(sig["act_took"], b, step.n + 1))
                    if x == 0:
                        dve.wait_ge(sig["q_filled"], at(sig["q_filled"], b, 16 * 9 * (a == 1)))
                    else:
                        dve.wait_ge(sig["k_filled"], at(sig["k_filled"], b, 0))
                    parts = v.qp if x == 0 else kp
                    split(lambda p3: parts[:, p3, :], v.lin[:], v.rest[:], sig["split_done"], 3 * q.n)
                elif q.kind == "v":
                    for k in range(NT):
                        ins = nc.vector.tensor_tensor(vx[1][:, k, :, 0:DK],
                                                      src[:, k * P:(k + 1) * P].rearrange("p (h d) -> p h d", d=DK),
                                                      R["bv1"].rearrange("p (h d) -> p h d", d=DK), ALU.add)
                    ins.then_inc(sig["dve_took"], 1)
                elif q.kind == "max":
                    dve.wait_ge(sig["max_scores"], at(sig["max_scores"], b, q.n + 1))
                    if a == 1:
                        h, k = divmod(x, NT)
                        if x % (HG * NT) == 0:
                            dve.wait_ge(sig["max_parts"], at(sig["max_parts"], b, 3 * find(st, "parts", 1, h // HG).n))
                        nc.vector.tensor_reduce(v.negmax[:, k, h % HG:h % HG + 1], src[:], AX.X, ALU.max,
                                                negate=True).then_inc(sig["max_taken"], 1)
                    else:
                        g, k = divmod(x, NT)
                        if x == 0:
                            dve.wait_ge(sig["max_parts"], at(sig["max_parts"], b, 0))
                        nc.vector.tensor_reduce(v.negmax[:, k, g * HG:(g + 1) * HG],
                                                src[:, 0:HG * SC].rearrange("p (h k) -> p h k", k=SC),
                                                AX.X, ALU.max, negate=True).then_inc(sig["max_taken"], 1)
                elif q.kind == "parts":
                    nh = HG if a == 1 else H
                    last = find(st, "max", a, (HG * NT * (x + 1) if a == 1 else G * NT) - 1)
                    dve.wait_ge(sig["max_taken"], at(sig["max_taken"], b, last.n + 1))
                    before = [s for s in STEPS[st] if s.kind == "rows"]
                    dve.wait_ge(sig["for_act"], at(sig["for_act"], b, before[q.n - 1].n + 1 if q.n else 0))
                    parts = v.negp[:].rearrange("p k a h -> p k (a h)")[:, :, 0:3 * nh]\
                        .rearrange("p k (a h) -> p k a h", a=3)
                    split(lambda p3: parts[:, :, p3, :], v.negmax[:, :, 0:nh], v.negrest[:, :, 0:nh],
                          sig["max_parts"], 3 * q.n)
                elif q.kind == "heads":
                    dve.wait_ge(sig["dve_took"], at(sig["dve_took"], b, q.n))
                    view = src[:].rearrange("p (t c j) -> p t c j", t=NT, j=32)
                    link(nc.vector.reciprocal(v.rden[:], view[:, :, :, DK]))
                    nc.vector.tensor_tensor(
                        v.z[:].rearrange("p t (g c d) -> p t g c d", g=G, d=DK)[:, :, x],
                        view[:, :, :, 0:DK], v.rden[:].unsqueeze(3).to_broadcast([P, NT, HG, DK]), ALU.mult)\
                        .then_inc(sig["dve_took"], 1)
                elif q.kind == "attn":
                    dve.wait_ge(sig["res_ready"], at(sig["res_ready"], b, find(st, "residual", a).n + 1))
                    dst = [x1, y, x3][a]
                    if st == 0 and section:
                        dve.wait_ge(sig1["base_ready"], at(sig1["base_ready"], b - 1, 1))
                        dve.wait_ge(sig1["z_ready"], at(sig1["z_ready"], b - 1, 1))
                    elif st == 1:
                        dve.wait_ge(sig1["stored"], at(sig1["stored"], b, 0))
                    nc.vector.tensor_tensor(dst[:], src[:].rearrange("p (t d) -> p t d", d=D), v.res[:], ALU.add)\
                        .then_inc(sig["dve_took"], 1)
                elif q.kind == "base":
                    dve.wait_ge(sig1["res_ready"], at(sig1["res_ready"], b, 0))
                    nc.vector.tensor_tensor(x2[:], x1[:], y[:], ALU.add).then_inc(sig1["base_ready"], 1)
                elif q.kind == "logit":
                    link(nc.vector.tensor_tensor(logit[:], src[:, 0:NT * NE].rearrange("p (t e) -> p t e", e=NE),
                                                 gate_b[:].unsqueeze(1).to_broadcast([P, NT, NE]), ALU.add))
                    link(nc.vector.tensor_reduce(top[:], logit[:], AX.X, ALU.max))
                    link(nc.vector.tensor_tensor(pick[:], logit[:], top[:].unsqueeze(2).to_broadcast([P, NT, NE]),
                                                 ALU.is_equal))
                    link(nc.vector.tensor_tensor(pick[:], pick[:],
                                                 falling[:].unsqueeze(1).to_broadcast([P, NT, NE]), ALU.mult))
                    link(nc.vector.tensor_reduce(top[:], pick[:], AX.X, ALU.max))
                    nc.vector.tensor_tensor(hot[:], falling[:].unsqueeze(1).to_broadcast([P, NT, NE]),
                                            top[:].unsqueeze(2).to_broadcast([P, NT, NE]), ALU.is_equal)\
                        .then_inc(sig1["dve_took"], 1)
                elif q.kind == "bias":
                    dve.wait_ge(sig1["base_ready"], at(sig1["base_ready"], b, 1))
                    nc.vector.tensor_tensor(x2[:], x2[:], src[:].rearrange("p (t d) -> p t d", d=D), ALU.add)\
                        .then_inc(sig1["dve_took"], 1)
                elif q.kind == "acc":
                    dve.wait_ge(sig1["down_done"], at(sig1["down_done"], b, NF * (x + 1)))
                    if x:
                        dve.wait_ge(sig1["acc_done"], at(sig1["acc_done"], b, x))
                    else:
                        dve.wait_ge(sig1["dve_took"], at(sig1["dve_took"], b, find(1, "bias").n + 1))
                    for k in range(NT):
                        ins = nc.vector.scalar_tensor_tensor(
                            out=x2[:, k, :], in0=v.acc[:, k * P:(k + 1) * P], scalar=hot[:, k, x:x + 1],
                            in1=x2[:, k, :], op0=ALU.mult, op1=ALU.add)
                    ins.then_inc(sig1["acc_done"], 1)
                elif q.kind == "score":
                    dve.wait_ge(sig1["z_ready"], at(sig1["z_ready"], b, 3))
                    for k in range(NT):
                        link(nc.vector.tensor_tensor(junk[:, 0:D], v.z[:, k, :], R["router"], ALU.mult))
                        ins = nc.vector.tensor_reduce(score[:, k:k + 1], junk[:, 0:D], AX.X, ALU.add)
                        if k + 1 < NT:
                            link(ins)
                    ins.then_inc(sig1["score_ready"], 1)
                elif q.kind == "rank":
                    dve.wait_ge(sig1["score_ready"], at(sig1["score_ready"], b, 1))
                    link(nc.vector.memset(counts[:], 0.0))
                    for k in range(NT):
                        own = score[:, k:k + 1]
                        if k:
                            link(nc.vector.tensor_scalar(junk[:, 0:k * P], src[:, 0:k * P], own, None,
                                                         ALU.is_ge, ALU.add, accum_out=counts[:, k, 0:1]))
                        link(nc.vector.tensor_scalar(junk[:, k * P:S], src[:, k * P:S], own, None,
                                                     ALU.is_gt, ALU.add, accum_out=counts[:, k, 1:2]))
                        link(nc.vector.scalar_tensor_tensor(out=junk[:, 0:P], in0=src[:, k * P:(k + 1) * P],
                                                            scalar=own, in1=lower[:], op0=ALU.is_equal, op1=ALU.mult))
                        link(nc.vector.tensor_reduce(counts[:, k, 2:3], junk[:, 0:P], AX.X, ALU.add))
                    nc.vector.tensor_reduce(rank[:], counts[:], AX.X, ALU.add).then_inc(sig1["dve_took"], 1)
                elif q.kind == "sum":
                    dve.wait_ge(sig1["sig_ready"], at(sig1["sig_ready"], b, 1))
                    dve.wait_ge(sig1["dve_took"], at(sig1["dve_took"], b, find(1, "rank").n + 1))
                    link(nc.vector.tensor_scalar(esig[:], esig[:], 1.0, None, ALU.add))
                    link(nc.vector.reciprocal(weight[:], esig[:]))
                    nc.vector.scalar_tensor_tensor(out=weight[:], in0=rank[:], scalar=float(TOPK) - 0.5,
                                                   in1=weight[:], op0=ALU.is_lt, op1=ALU.mult)\
                        .then_inc(sig1["weight_ready"], 1)
                    link(nc.vector.tensor_tensor(x3[:], x3[:], v.z[:], ALU.add))
                    dve.wait_ge(sig1["down_done"], at(sig1["down_done"], b, NF * NE + NF))
                    nc.vector.tensor_tensor(junk[:].rearrange("p (t d) -> p t d", d=D),
                                            v.acc[:].rearrange("p (t d) -> p t d", d=D),
                                            R["fb2"].unsqueeze(1).to_broadcast([P, NT, D]), ALU.add)\
                        .then_inc(sig1["summed"], 1)
                elif q.kind == "out":
                    dve.wait_ge(sig1["weight_ready"], at(sig1["weight_ready"], b, 1))
                    dve.wait_ge(sig1["summed"], at(sig1["summed"], b, 1))
                    for k in range(NT):
                        ins = nc.vector.scalar_tensor_tensor(
                            out=x3[:, k, :], in0=junk[:, k * P:(k + 1) * P], scalar=weight[:, k:k + 1],
                            in1=x3[:, k, :], op0=ALU.mult, op1=ALU.add)
                    ins.then_inc(sig1["out_ready"], 1)

            run(dve, body)
            assert links[1] == LINKS, links


def shape_constants():
    import numpy as np

    bf = np.dtype("bfloat16")

    def parts(a):
        out, rest = [], a.astype(np.float32)
        for _ in range(3):
            p = rest.astype(bf)
            out.append(p)
            rest = rest - p.astype(np.float32)
        return out

    slope = np.array([2.0 ** (-8.0 * (h + 1) / H) for h in range(H)], np.float32)
    eye = np.eye(SC, dtype=np.float32)
    keys, toks = np.arange(SC, dtype=np.float32), np.arange(S, dtype=np.float32)
    k_lin = parts(-slope[:, None] * (keys + (S - SC))[None, :])
    q_lin = parts(slope[:, None] * toks[None, :])
    one_k, one_q = np.ones((H, SC), bf), np.ones((H, S), bf)
    toks3 = toks[S - P:]
    return {
        "ident": np.eye(P, dtype=np.float32),
        "identb": np.eye(P).astype(bf),
        "eye4": np.ascontiguousarray(np.repeat(eye[:, None, :], HG, 1)).astype(bf),
        "slopes": np.stack([(eye[:, None, :] * p.astype(np.float32)[None, :, None]).astype(bf)
                            for p in parts(-2 * slope)], 1),
        "corner": np.maximum(0, toks3[None, :] - keys[:, None] - (S - SC)).astype(bf),
        "lower": (np.arange(P)[None, :] < np.arange(P)[:, None]).astype(np.float32),
        "falling": np.tile(np.arange(NE, 0, -1).astype(np.float32), (P, 1)),
        "halfneg": np.full((P, NT), -0.5, np.float32),
        "kones": np.ones((3, H, S), bf),
        "kalibi": np.stack(k_lin + [one_k] * 3),
        "qalibi": np.stack([one_q] * 3 + q_lin),
    }


def kernel(**inputs):
    import numpy as np
    import concourse.bacc as bacc
    from concourse.bass_utils import run_bass_kernel_spmd

    a = {k: np.asarray(v) for k, v in inputs.items()}
    dh = np.arange(D).reshape(H, DK).T.reshape(-1)
    x0, f0, x1, f1 = "L0_xattn_", "L0_ffn_", "L1_xattn_", "L1_ffn_"
    wkv, bkv = a[x1 + "Wkv"], a[x1 + "bkv"]
    w = [a[x0 + "W_q"].T[:, dh], a[x0 + "W_k"].T[:, dh], a[x0 + "W_v"].T, a[x0 + "W_o"].T,
         a[f0 + "wq"][:, dh], a[f0 + "wk"][:, dh], a[f0 + "wv"], a[f0 + "wo"],
         a[x1 + "Wq"][:, dh], wkv[:, :D][:, dh], wkv[:, D:], a[x1 + "Wo"]]
    c = [a[x0 + "b_q"][dh], a[x0 + "b_k"][dh], a[f0 + "bq"][dh], a[f0 + "bk"][dh], a[x1 + "bq"][dh], bkv[:D][dh],
         a[f0 + "ln1_g"], a[f0 + "ln1_b"], a[f0 + "ln2_g"], a[f0 + "ln2_b"]]
    r = [a[x0 + "b_v"], a[x0 + "b_o"], a[f0 + "bv"], a[f0 + "bo"], bkv[D:], a[x1 + "bo"], a[f1 + "b2"],
         a[f1 + "w_router"]]
    arrays = {
        "x": a["x"], "ctx": a["ctx_1024"], "mask": a["mask_Bx1xSxS2_ik1"],
        "w": np.stack(w, 1), "c": np.stack(c, 1), "r": np.stack(r, 0),
        "gate_w": a[f0 + "gate_w"], "gate_b": a[f0 + "gate_b"],
        "w1": a[f0 + "w1"].transpose(1, 0, 2),
        "b1": a[f0 + "b1"].reshape(NE, NF, P).transpose(2, 0, 1),
        "w2": a[f0 + "w2"].reshape(NE, NF, P, D).transpose(2, 0, 1, 3),
        "b2": a[f0 + "b2"],
        "fw1": a[f1 + "W1"], "fb1": a[f1 + "b1"].reshape(NF, P).T,
        "fw2": a[f1 + "W2"].reshape(NF, P, D).transpose(1, 0, 2),
    }
    arrays.update(shape_constants())
    arrays = {k: np.ascontiguousarray(v) for k, v in arrays.items()}
    nc = bacc.Bacc("TRN2", target_bir_lowering=False, num_devices=1)
    tensors = {k: nc.dram_tensor(f"in_{k}", v.shape, mybir.dt.from_np(v.dtype), kind="ExternalInput").ap()
               for k, v in arrays.items()}
    tensors["out"] = nc.dram_tensor("out_dram", (B, S, D), F32, kind="ExternalOutput").ap()
    build(nc, tensors)
    result = run_bass_kernel_spmd(nc, [{f"in_{k}": v for k, v in arrays.items()}], core_ids=[0])
    return result.results[0]["out_dram"]
```
